# Optimizing a Trainium2 kernel written in Bass

```python
import numpy as np
import jax
import jax.numpy as jnp

def _softmax(x, axis=-1):
    return jax.nn.softmax(x, axis=axis)

def _gelu(x):
    return jax.nn.gelu(x, approximate=True)

def _silu(x):
    return jax.nn.silu(x)

def _sigmoid(x):
    return jax.nn.sigmoid(x)

def _layernorm(x, axis=-1, eps=1e-05):
    m = jnp.mean(x, axis=axis, keepdims=True)
    v = jnp.var(x, axis=axis, keepdims=True)
    return (x - m) / jnp.sqrt(v + eps)

def _scatter_add(tgt, idx, src, axis=0):
    return tgt.at[idx].add(src)

def _segment_sum(src, seg, n):
    return jax.ops.segment_sum(src, seg, n)
kernel_name = 'mk_xattn_ffn_d1_seqx_r2_58cb96'

def setup_inputs(seed: int=0):
    np.random.seed(seed)
    _w = jnp.asarray

    def _rec_inputs():
        import jax
        import jax.numpy as jnp
        _rk = jax.random.key(seed)
        x = 7.22e-05 + 1 * jax.random.normal(jax.random.fold_in(_rk, 1), (2, 2048, 512), jnp.float32)
        _lenS = 2048 - jax.random.randint(jax.random.fold_in(_rk, 7), (2,), 0, max(1, 2048 // 4) + 1, jnp.int32)
        _lenS2 = 77 - jax.random.randint(jax.random.fold_in(_rk, 8), (2,), 0, max(1, 77 // 4) + 1, jnp.int32)
        _ctx_768P = jax.random.normal(jax.random.fold_in(_rk, 11), (2, 16, 384), jnp.float32)
        _ctx_768c = jax.random.dirichlet(jax.random.fold_in(_rk, 511), 0.3 * jnp.ones((16,), jnp.float32), (2, 77))
        _ctx_768t = jnp.einsum('bsk,bkd->bsd', _ctx_768c, _ctx_768P)
        _ctx_768t = _ctx_768t * jax.lax.rsqrt(jnp.mean(jnp.square(_ctx_768t)) + 1e-12) * 0.953939
        ctx_768 = -0.000191848 + 0.999787 * (_ctx_768t + 0.3 * jax.random.normal(jax.random.fold_in(_rk, 611), (2, 77, 384), jnp.float32))
        return (x, ctx_768)
    x, ctx_768 = _rec_inputs()

    def _L0_xattn_setup():
        import jax, jax.numpy as jnp
        import numpy as np
        NUM_HEADS = 16
        CLAMP = 10000.0
        key = jax.random.key(seed)
        ks = jax.random.split(key, 8)
        B, Nq, Nkv, Cq, Ckv = (4, 1024, 1024, 512, 384)
        s_q = 1.0 / np.sqrt(Cq)
        s_kv = 1.0 / np.sqrt(Ckv)
        return {'query': jax.random.normal(ks[0], (B, Nq, Cq), jnp.float32), 'key_value': jax.random.normal(ks[1], (B, Nkv, Ckv), jnp.float32), 'Wq': jax.random.normal(ks[2], (Cq, Cq), jnp.float32) * s_q, 'bq': jnp.zeros((Cq,), jnp.float32), 'Wk': jax.random.normal(ks[3], (Ckv, Cq), jnp.float32) * s_kv, 'bk': jnp.zeros((Cq,), jnp.float32), 'Wv': jax.random.normal(ks[4], (Ckv, Cq), jnp.float32) * s_kv, 'bv': jnp.zeros((Cq,), jnp.float32), 'Wo': jax.random.normal(ks[5], (Cq, Cq), jnp.float32) * s_q, 'bo': jnp.zeros((Cq,), jnp.float32)}
    _L0_xattn_all = _L0_xattn_setup()
    _L0_xattn_in = {k: v for k, v in _L0_xattn_all.items() if k in ('Wq', 'bq', 'Wk', 'bk', 'Wv', 'bv', 'Wo', 'bo')}
    del _L0_xattn_all

    def _L0_ffn_setup():
        import jax, jax.numpy as jnp
        import numpy as np
        D_MODEL, D_FF, RANK = (512, 2048, 128)
        B, S = (4, 2048)
        key = jax.random.key(seed)
        ks = jax.random.split(key, 7)
        return {'x': jax.random.normal(ks[0], (B, S, D_MODEL), dtype=jnp.float32), 'U1': jax.random.normal(ks[1], (D_MODEL, RANK), dtype=jnp.float32) * 0.02, 'V1': jax.random.normal(ks[2], (RANK, D_FF), dtype=jnp.float32) * 0.02, 'b1': jnp.zeros((D_FF,), dtype=jnp.float32), 'U2': jax.random.normal(ks[3], (D_FF, RANK), dtype=jnp.float32) * 0.02, 'V2': jax.random.normal(ks[4], (RANK, D_MODEL), dtype=jnp.float32) * 0.02, 'b2': jnp.zeros((D_MODEL,), dtype=jnp.float32)}
    _L0_ffn_all = _L0_ffn_setup()
    _L0_ffn_in = {k: v for k, v in _L0_ffn_all.items() if k in ('U1', 'V1', 'b1', 'U2', 'V2', 'b2')}
    del _L0_ffn_all
    return {'x': x, 'ctx_768': ctx_768, 'L0_xattn_Wq': _L0_xattn_in['Wq'], 'L0_xattn_bq': _L0_xattn_in['bq'], 'L0_xattn_Wk': _L0_xattn_in['Wk'], 'L0_xattn_bk': _L0_xattn_in['bk'], 'L0_xattn_Wv': _L0_xattn_in['Wv'], 'L0_xattn_bv': _L0_xattn_in['bv'], 'L0_xattn_Wo': _L0_xattn_in['Wo'], 'L0_xattn_bo': _L0_xattn_in['bo'], 'L0_ffn_U1': _L0_ffn_in['U1'], 'L0_ffn_V1': _L0_ffn_in['V1'], 'L0_ffn_b1': _L0_ffn_in['b1'], 'L0_ffn_U2': _L0_ffn_in['U2'], 'L0_ffn_V2': _L0_ffn_in['V2'], 'L0_ffn_b2': _L0_ffn_in['b2']}

def reference(x, ctx_768, L0_xattn_Wq, L0_xattn_bq, L0_xattn_Wk, L0_xattn_bk, L0_xattn_Wv, L0_xattn_bv, L0_xattn_Wo, L0_xattn_bo, L0_ffn_U1, L0_ffn_V1, L0_ffn_b1, L0_ffn_U2, L0_ffn_V2, L0_ffn_b2):
    import jax
    import jax.numpy as jnp

    def _L0_xattn_ref(query, key_value, Wq, bq, Wk, bk, Wv, bv, Wo, bo):
        import jax, jax.numpy as jnp
        import numpy as np
        NUM_HEADS = 16
        CLAMP = 10000.0
        B, Nq, Cq = query.shape
        Nkv = key_value.shape[1]
        H = NUM_HEADS
        D = Cq // H
        scale = D ** (-0.5)
        q = (query @ Wq + bq).reshape(B, Nq, H, D).transpose(0, 2, 1, 3)
        k = (key_value @ Wk + bk).reshape(B, Nkv, H, D).transpose(0, 2, 1, 3)
        v = (key_value @ Wv + bv).reshape(B, Nkv, H, D).transpose(0, 2, 1, 3)
        attn = jnp.einsum('bhqd,bhkd->bhqk', q, k) * scale
        attn = jnp.clip(attn, -CLAMP, CLAMP)
        attn = jax.nn.softmax(attn, axis=-1)
        attn = jnp.where(jnp.any(jnp.isnan(attn)), jnp.asarray(1.0 / Nkv, attn.dtype), attn)
        x = jnp.einsum('bhqk,bhkd->bqhd', attn, v).reshape(B, Nq, Cq)
        return x @ Wo + bo

    def _L0_ffn_ref(x, U1, V1, b1, U2, V2, b2):
        import jax, jax.numpy as jnp
        import numpy as np
        D_MODEL, D_FF, RANK = (512, 2048, 128)
        B, S = (4, 2048)
        P = jnp.einsum('bsd,dr->bsr', x, U1)
        H = jax.nn.gelu(jnp.einsum('bsr,rf->bsf', P, V1) + b1)
        Q = jnp.einsum('bsf,fr->bsr', H, U2)
        return jnp.einsum('bsr,rd->bsd', Q, V2) + b2
    x = x + _L0_xattn_ref(_layernorm(x, axis=-1), ctx_768, L0_xattn_Wq, L0_xattn_bq, L0_xattn_Wk, L0_xattn_bk, L0_xattn_Wv, L0_xattn_bv, L0_xattn_Wo, L0_xattn_bo)
    x = x + _L0_ffn_ref(_layernorm(x, axis=-1), L0_ffn_U1, L0_ffn_V1, L0_ffn_b1, L0_ffn_U2, L0_ffn_V2, L0_ffn_b2)
    return x

_drawn_inputs = setup_inputs


def setup_inputs(seed=0):
    import zlib

    import numpy as np

    out = dict(_drawn_inputs(seed))
    spreads = {'L0_xattn_bq': (0.0, 0.393),
     'L0_xattn_bk': (0.0, 2.0),
     'L0_xattn_bv': (0.0, 0.1),
     'L0_xattn_bo': (0.0, 0.1),
     'L0_ffn_b1': (0.0, 0.8),
     'L0_ffn_b2': (0.0, 0.8)}
    factors = {'L0_ffn_U1': 6.158, 'L0_ffn_V1': 6.18, 'L0_ffn_U2': 4.366, 'L0_ffn_V2': 4.899}
    for name, (base, spread) in spreads.items():
        noise = np.random.default_rng([zlib.crc32(name.encode()), seed]).standard_normal(out[name].shape)
        drawn = base * np.exp(spread * noise) if base else spread * noise
        out[name] = jnp.asarray(drawn.astype(out[name].dtype))
    for name, factor in factors.items():
        out[name] = (out[name] * factor).astype(out[name].dtype)
    return out
```

```python
import concourse.bass as bass
from concourse import mybir
from contextlib import ExitStack

F32 = mybir.dt.float32
F32R = mybir.dt.float32r
ALU = mybir.AluOpType
ACT = mybir.ActivationFunctionType
AX = mybir.AxisListType

P = 128
B, S, D = 2, 2048, 512
KV, CKV = 77, 384
H = 16
DH = D // H
GH = P // DH
G = H // GH
GW = GH * KV
HKV = H * KV
NCH = -(-HKV // P)
KD = D // P
KC = CKV // P
R, FF = 128, 2048
NFF = FF // P
EPS = 1e-5
CLAMP = 10000.0
SCALE = DH ** -0.5
PAIRS = [(c, g) for g in range(G) for c in range(NCH) if c * P < (g + 1) * GW and (c + 1) * P > g * GW]
NP = len(PAIRS)

TA = 256
NA = B * S // TA
TPB = S // P
TB = 512
UB = TB // P
NB = B * S // TB


def num(j, b, d=0):
    return 2 * j + (b + d)


def there(total, j, b, d):
    return not isinstance(j, int) or 0 <= 2 * j + b + d < total


def shift(j, b, d):
    return j + (b + d) // 2, (b + d) % 2


def until(eng, sem, value):
    if not isinstance(value, int) or value > 0:
        eng.wait_ge(sem, value)


def pairs(eng, total, body):
    head = 2 if total > 8 else 1
    for j in range(head):
        body(j)
    with eng.Fori(head, total // 2 - 1) as j:
        body(j)
    body(total // 2 - 1)
    body(total // 2)


def xattn_ffn(nc, x, ctx, wq, bq, wk, bk, wv, bv, wo, bo, u1, v1, b1, u2, v2, b2, out):
    x_t = x.rearrange("b (t p) d -> (b t) p d", p=P)
    y_dram = nc.dram_tensor("y_between", [B * S, D], F32).ap()
    y_t = y_dram.rearrange("(t p) d -> t p d", p=P)
    y_b = y_dram.rearrange("(n t p) d -> n p t d", p=P, t=UB)
    out_t = out.rearrange("b (t p) d -> (b t) p d", p=P)

    stack = ExitStack()
    with stack:
        def sb(name, shape, dt=F32):
            return stack.enter_context(nc.sbuf_tensor(name, shape, dt))

        def sem(name):
            return stack.enter_context(nc.semaphore(name))

        wqo_r = sb("wqo_r", [P, 2 * 2 * KD * D], F32R)
        wq_r = wqo_r[:, 0:2 * KD * D].rearrange("p (h k n) -> p h k n", h=2, k=KD)
        wo_r = wqo_r[:, 2 * KD * D:].rearrange("p (h k n) -> p h k n", h=2, k=KD)
        kb_t = sb("kblk_r", [P, B * 2 * G * GW], F32R)
        kblk = kb_t[:, :].rearrange("p (b h g w) -> p b h g w", b=B, h=2, g=G)
        vb_t = sb("vblk_r", [P, B * 2 * NP * P], F32R)
        vblk = vb_t[:, :].rearrange("p (b h c n) -> p b h c n", b=B, h=2, c=NP)
        zt_t = sb("zt_r", [P, 2 * KD * TA], F32R)
        zt = zt_t[:, :].rearrange("p (h k t) -> p h k t", h=2, k=KD)
        qt_t = sb("qt_r", [P, 2 * 2 * G * TA], F32R)
        qt = qt_t[:, :].rearrange("p (b h g t) -> p b h g t", b=2, h=2, g=G)
        ot = sb("ot_r", [P, 2, G, TA], F32R)
        pt_t = sb("pt_r", [P, 2 * NCH * TA], F32R)
        pt = pt_t[:, :].rearrange("p (h c t) -> p h c t", h=2, c=NCH)
        v1_r = wqo_r[:, 0:2 * FF].rearrange("p (h n) -> p h n", h=2)
        u1_r = wqo_r[:, 2 * FF:2 * FF + 2 * KD * R].rearrange("p (h k n) -> p h k n", h=2, k=KD)
        v2_r = wqo_r[:, 2 * FF + 2 * KD * R:2 * FF + 2 * KD * R + 2 * D].rearrange("p (h n) -> p h n", h=2)
        u2_r = kb_t[:, 0:2 * NFF * R].rearrange("p (h k n) -> p h k n", h=2, k=NFF)
        z2t = qt_t[:, :].rearrange("p (h k t) -> p h k t", h=2, k=KD)
        p1t = zt_t[:, :].rearrange("p (b h t) -> p b h t", b=2, h=2)
        hs = pt_t[:, 0:8 * TB].rearrange("p (s h t) -> p s h t", s=4, h=2)
        q2t = pt_t[:, 8 * TB:10 * TB].rearrange("p (h t) -> p h t", h=2)

        xs = sb("xs", [P, 8 * D])
        xa = xs[:, 0:4 * D].rearrange("p (s d) -> p s d", s=4)
        xb = xs[:, 4 * D:].rearrange("p (s d) -> p s d", s=4)
        yb = xs[:, :].rearrange("p (b t d) -> p b t d", b=2, t=UB)
        ss = sb("ss", [P, 4 * NCH * P])
        sc = ss[:, :].rearrange("p (s w) -> p s w", s=4)
        hg = ss[:, 0:4 * TB].rearrange("p (s t) -> p s t", s=4)
        z2 = ss[:, 4 * TB:4 * TB + UB * D].rearrange("p (t d) -> p t d", t=UB)
        fw = sb("fw", [P, 2 * FF + KD * R + D])
        z = sb("z", [P, 2, D])
        wq_f = ss[:, 0:KD * D].rearrange("p (k n) -> p k n", k=KD)
        wv_f = ss[:, KD * D:KD * D + KC * D].rearrange("p (k n) -> p k n", k=KC)
        ctx_f = ss[0:KV, (KD + KC) * D:(KD + KC) * D + B * CKV].rearrange("p (b c) -> p b c", b=B)
        wo_f = xb.rearrange("p k n -> p k n")
        vpl_f = fw[:, 0:B * NP * P].rearrange("p (b c n) -> p b c n", b=B, c=NP)
        wk_f = fw[:, B * NP * P:B * NP * P + KC * D].rearrange("p (k n) -> p k n", k=KC)
        ctxt_f = sb("ctxt_f", [P, KC, B, KV])
        kt_f = sb("kt_f", [P, G, B, KV])
        v_f = sb("v_f", [KV, B, D])
        v1_f = fw[:, 0:FF]
        u2_f = fw[:, FF:2 * FF].rearrange("p (k n) -> p k n", k=NFF)
        u1_f = fw[:, 2 * FF:2 * FF + KD * R].rearrange("p (k n) -> p k n", k=KD)
        v2_f = fw[:, 2 * FF + KD * R:]
        ya = fw[:, 0:2 * UB * D].rearrange("p (b t d) -> p b t d", b=2, t=UB)
        bias_row = sb("bias_row", [P, D])
        bias_f = sb("bias_f", [2 * G + NFF, P])
        bqs_c = sb("bqs_c", [P, G])
        bk_c = sb("bk_c", [P, G])
        b1_c = sb("b1_c", [P, NFF])
        ident = sb("ident", [P, P])
        mhalf = sb("mhalf", [P, UB])
        eps_c = sb("eps_c", [P, UB])
        stall = sb("stall", [P, 1])
        stats = sb("stats", [P, 4, 6])
        mv = sb("mv", [P, 4, 2])
        var_e = sb("var_e", [P, 4])
        rstd = sb("rstd", [P, 4])
        smax = sb("smax", [P, 4, H])
        ssum = sb("ssum", [P, 4, H])
        rsum = sb("rsum", [P, 4, H])

        bank = [stack.enter_context(nc.psum_tensor(f"bank{i}", [P, 512], F32)) for i in range(4, 8)]
        ps_s = stack.enter_context(nc.psum_tensor("ps_s", [P, 4, 512], F32))
        B4, B5, B6, B7 = bank

        in_x = [sem(f"in_x{i}") for i in range(4)]
        in_xb = [sem(f"in_xb{i}") for i in range(4)]
        y_out = [sem(f"y_out{i}") for i in range(4)]
        in_wq, in_wk, in_wv, in_wo, in_ctx = (sem(n) for n in ("in_wq", "in_wk", "in_wv", "in_wo", "in_ctx"))
        in_bias, in_bv, in_bo, in_b2, bias_turned = (sem(n) for n in ("in_bias", "in_bv", "in_bo", "in_b2", "bias_turned"))
        in_ffn, v_placed = sem("in_ffn"), sem("v_placed")
        const_ready, zeroed = sem("const_ready"), sem("zeroed")
        ctx_turned, ctx_copied, k_full, v_full, k_copied, v_copied = (
            sem(n) for n in ("ctx_turned", "ctx_copied", "k_full", "v_full", "k_copied", "v_copied"))
        wq_hi, wq_lo, wo_hi, wo_lo, kb_hi, kb_lo, vb_hi, vb_lo, pad_zero, bqs_ready = (
            sem(n) for n in ("wq_hi", "wq_lo", "wo_hi", "wo_lo", "kb_hi", "kb_lo", "vb_hi", "vb_lo",
                             "pad_zero", "bqs_ready"))
        stats_done, mv_done, var_done, rstd_done, z_done = (
            sem(n) for n in ("stats_done", "mv_done", "var_done", "rstd_done", "z_done"))
        zt_full, zt_hi, zt_lo, q_full, q_hi, q_lo = (
            sem(n) for n in ("zt_full", "zt_hi", "zt_lo", "q_full", "q_hi", "q_lo"))
        s_full, s_clip, s_max, s_sub, s_exp, s_sum, s_rec, s_norm = (
            sem(n) for n in ("s_full", "s_clip", "s_max", "s_sub", "s_exp", "s_sum", "s_rec", "s_norm"))
        pt_full, pt_hi, pt_lo, pv_full, ot_hi, ot_lo, o_full, xb_done, y_done = (
            sem(n) for n in ("pt_full", "pt_hi", "pt_lo", "pv_full", "ot_hi", "ot_lo", "o_full",
                             "xb_done", "y_done"))
        ffn_hi, ffn_lo = sem("ffn_hi"), sem("ffn_lo")
        in_y = [sem(f"in_y{i}") for i in range(2)]
        outs = [sem(f"outs{i}") for i in range(2)]
        stats2, mv2, var2, rstd2, z2_done, yb_done = (
            sem(n) for n in ("stats2", "mv2", "var2", "rstd2", "z2_done", "yb_done"))
        z2t_full, z2t_hi, z2t_lo, p1_full, p1_hi, p1_lo = (
            sem(n) for n in ("z2t_full", "z2t_hi", "z2t_lo", "p1_full", "p1_hi", "p1_lo"))
        h_full, h_gelu, h_hi, h_lo, h_lo_pool, u2_done, q2_hi, q2_lo, o2_full, o2_done = (
            sem(n) for n in ("h_full", "h_gelu", "h_hi", "h_lo", "h_lo_pool", "u2_done", "q2_hi", "q2_lo",
                             "o2_full", "o2_done"))

        PASSES = ((0, 0), (0, 1), (1, 0))

        def tile_row(j, b, u):
            return 2 * j + (b * TPB + u)

        def v_pieces(h):
            r, end = h * KV, (h + 1) * KV
            while r < end:
                c = r // P
                n = min(end, (c + 1) * P) - r
                yield PAIRS.index((c, h // GH)), r % P, r - h * KV, n
                r += n

        N_PIECES = sum(len(list(v_pieces(h))) for h in range(H))

        block = stack.enter_context(nc.Block())

        @block.sync
        def _(sp):
            def held(value):
                return value if isinstance(value, int) else sp.snap(value)

            def load_x(j, b):
                jj, bb = j, b
                for u in range(2):
                    k = 2 * bb + u
                    row = held(tile_row(jj, bb, u))
                    until(sp, z_done, 2 * (2 * jj + bb - 2) + u + 1)
                    sp.dma_start(xa[:, k, :], x_t[row, :, :]).then_inc(in_x[k], 16)

            load_x(0, 0)
            sp.dma_start(wq_f, wq.rearrange("(k p) n -> p k n", p=P)).then_inc(in_wq, 16)
            load_x(0, 1)
            sp.dma_start(wk_f, wk.rearrange("(k p) n -> p k n", p=P)).then_inc(in_wk, 16)
            sp.dma_start(wv_f, wv.rearrange("(k p) n -> p k n", p=P)).then_inc(in_wv, 16)
            sp.dma_start(wo_f, wo.rearrange("(k p) n -> p k n", p=P)).then_inc(in_wo, 16)
            sp.wait_ge(v_copied, 2)
            sp.wait_ge(zeroed, 2)
            for h in range(H):
                for c, p0, kv0, n in v_pieces(h):
                    d0 = (h % GH) * DH
                    sp.dma_start(vpl_f[p0:p0 + n, :, c, d0:d0 + DH],
                                 v_f[kv0:kv0 + n, :, h * DH:(h + 1) * DH]).then_inc(v_placed, 16)
            load_x(1, 0)
            sp.wait_ge(vb_lo, 1)
            sp.wait_ge(k_full, 1)
            sp.dma_start(v1_f, v1).then_inc(in_ffn, 16)
            sp.dma_start(u2_f, u2.rearrange("(k p) n -> p k n", p=P)).then_inc(in_ffn, 16)
            sp.dma_start(u1_f, u1.rearrange("(k p) n -> p k n", p=P)).then_inc(in_ffn, 16)
            sp.dma_start(v2_f, v2).then_inc(in_ffn, 16)
            sp.wait_ge(wo_lo, 1)

            def body(j):
                for b in range(2):
                    if there(NA, j, b, 3):
                        load_x(*shift(j, b, 3))
                    if there(NA, j, b, -2):
                        for u in range(2):
                            k = 2 * b + u
                            row = held(tile_row(j - 1, b, u))
                            sp.wait_ge(y_done, 2 * num(j, b, -2) + u + 1)
                            sp.dma_start(y_t[row, :, :], xb[:, k, :]).then_inc(y_out[k], 16)
                    if there(NA, j, b, 0):
                        for u in range(2):
                            k = 2 * b + u
                            row = held(tile_row(j, b, u))
                            until(sp, y_out[k], 16 * j)
                            sp.dma_start(xb[:, k, :], x_t[row, :, :]).then_inc(in_xb[k], 16)

            pairs(sp, NA, body)

            def y_block(j, b):
                return j + b * (S // TB)

            def load_y(j, b):
                at, used = held(y_block(j, b)), held(UB * (2 * j + b - 1))
                until(sp, z2_done, used)
                until(sp, yb_done, used)
                sp.dma_start(ya[:, b, :, :], y_b[at, :, :, :]).then_inc(in_y[b], 16)

            sp.wait_ge(ffn_lo, 4)
            for k in range(4):
                sp.wait_ge(y_out[k], 16 * (NA // 2))
            load_y(0, 0)
            load_y(0, 1)

            def body2(j):
                for b in range(2):
                    if there(NB, j, b, 2):
                        load_y(j + 1, b)
                    if there(NB, j, b, -1):
                        jj, bb = shift(j, b, -1)
                        for t in range(UB):
                            row = held(UB * jj + (bb * TPB + t))
                            sp.wait_ge(o2_done, UB * num(j, b, -1) + t + 1)
                            sp.dma_start(out_t[row, :, :], yb[:, bb, t, :])\
                              .then_inc(outs[bb], 16)

            pairs(sp, NB, body2)
            for b in range(2):
                sp.wait_ge(outs[b], 16 * UB * (NB // 2))

        @block.gpsimd
        def _(pool):
            pool.memset(ident[:, :], 0.0).then_inc(const_ready, 1)
            pool.memset(mhalf[:, :], -0.5).then_inc(const_ready, 1)
            pool.memset(eps_c[:, :], EPS).then_inc(const_ready, 1)
            pool.wait_ge(const_ready, 3)
            pool.affine_select(out=ident[:, :], in_=ident[:, :], compare_op=ALU.not_equal, fill=1.0,
                               base=0, pattern=[[-1, P]], channel_multiplier=1).then_inc(const_ready, 1)

            def rstd_of(j, b):
                n = 2 * j + b
                pool.wait_ge(mv_done, 2 * n + 2)
                until(pool, z_done, 2 * n - 2)
                pool.tensor_tensor(var_e[:, 2 * b:2 * b + 2], mv[:, 2 * b:2 * b + 2, 1], eps_c[:, 0:2],
                                   ALU.add).then_inc(var_done, 1)
                pool.wait_ge(var_done, n + 1)
                pool.tensor_tensor(rstd[:, 2 * b:2 * b + 2], var_e[:, 2 * b:2 * b + 2], mhalf[:, 0:2],
                                   ALU.pow).then_inc(rstd_done, 1)

            rstd_of(0, 0)
            pool.memset(kb_t[:, :].bitcast(F32), 0.0).then_inc(zeroed, 1)
            rstd_of(0, 1)
            pool.memset(vpl_f, 0.0).then_inc(zeroed, 1)
            rstd_of(1, 0)

            def heads(t, k):
                return t[:, k, 0:HKV].rearrange("p (h w) -> p h w", h=H)

            def subtract_max(j, b, u):
                k = 2 * b + u
                pool.wait_ge(s_max, 2 * num(j, b) + u + 1)
                pool.tensor_tensor(heads(sc, k), heads(sc, k),
                                   smax[:, k, :].unsqueeze(2).broadcast_to([P, H, KV]),
                                   ALU.subtract).then_inc(s_sub, 1)

            def normalise(j, b, u):
                k = 2 * b + u
                pool.wait_ge(s_rec, 2 * num(j, b) + u + 1)
                pool.tensor_tensor(heads(sc, k), heads(sc, k),
                                   rsum[:, k, :].unsqueeze(2).broadcast_to([P, H, KV]),
                                   ALU.mult).then_inc(s_norm, 1)

            def x_plus_bo(j, b, u):
                k = 2 * b + u
                pool.wait_ge(in_xb[k], 16 * (j + 1))
                pool.tensor_tensor(xb[:, k, :], xb[:, k, :], bias_row[:, :], ALU.add).then_inc(xb_done, 1)

            pool.wait_ge(in_bo, 16)

            def body(j):
                for b in range(2):
                    if there(NA, j, b, -1):
                        normalise(*shift(j, b, -1), 1)
                    if there(NA, j, b, 0):
                        subtract_max(j, b, 0)
                    if there(NA, j, b, -1):
                        x_plus_bo(*shift(j, b, -1), 0)
                        x_plus_bo(*shift(j, b, -1), 1)
                    if there(NA, j, b, 0):
                        subtract_max(j, b, 1)
                        normalise(j, b, 0)
                    if there(NA, j, b, 3):
                        rstd_of(*shift(j, b, 3))

            pairs(pool, NA, body)

            def rstd2_of(j, b):
                n = 2 * j + b
                pool.wait_ge(mv2, UB * (n + 1))
                until(pool, z2_done, UB * n)
                pool.tensor_tensor(var_e[:, :], mv[:, :, 1], eps_c[:, :], ALU.add).then_inc(var2, 1)
                pool.wait_ge(var2, n + 1)
                pool.tensor_tensor(rstd[:, :], var_e[:, :], mhalf[:, :], ALU.pow).then_inc(rstd2, 1)

            def y_plus_b2(j, b, t):
                if t == 0:
                    pool.wait_ge(in_y[b], 16 * (j + 1))
                    until(pool, outs[b], 16 * UB * j)
                pool.tensor_tensor(yb[:, b, t, :], ya[:, b, t, :], bias_row[:, :], ALU.add).then_inc(yb_done, 1)

            pool.wait_ge(z_done, 2 * NA)
            for k in range(4):
                pool.wait_ge(y_out[k], 16 * (NA // 2))
            rstd2_of(0, 0)
            pool.wait_ge(in_b2, 16)
            for t in range(UB):
                y_plus_b2(0, 0, t)
            rstd2_of(0, 1)

            def body2(j):
                for b in range(2):
                    for c in range(NFF):
                        if c % 2 and there(NB, j, b, 0):
                            n = 16 * num(j, b) + c
                            pool.wait_ge(h_hi, n + 1)
                            pool.tensor_tensor(hs[:, c % 4, 1, :], hg[:, c % 4, :],
                                               hs[:, c % 4, 0, :].bitcast(F32), ALU.subtract)\
                                .then_inc(h_lo_pool, 1)
                        if c == 11 and there(NB, j, b, 2):
                            rstd2_of(j + 1, b)
                        if c in (12, 13, 14, 15) and there(NB, j, b, 1):
                            y_plus_b2(*shift(j, b, 1), c - 12)

            pairs(pool, NB, body2)

        @block.scalar
        def _(act):
            act.dma_start(ctx_f, ctx.rearrange("b k c -> k b c")).then_inc(in_ctx, 16)
            for row, v in ((0, bq), (G, bk), (2 * G, b1)):
                n = v.shape[0] // P
                act.dma_start(bias_f[row:row + n, :], v.rearrange("(g p) -> g p", p=P)).then_inc(in_bias, 16)
            act.dma_start(bias_row[:, :], bv.partition_broadcast(P)).then_inc(in_bv, 16)

            def turned_z(j, b):
                n = 2 * j + b
                for u, bk_ in ((0, B6), (1, B4)):
                    act.wait_ge(zt_full, 2 * n + u + 1)
                    act.activation(zt[:, 0, :, u * P:(u + 1) * P],
                                   bk_[:, :].rearrange("p (k t) -> p k t", k=KD), ACT.Copy).then_inc(zt_hi, 1)

            def q_high(j, b, half):
                n = 2 * j + b
                act.wait_ge(q_full, 2 * n + half + 1)
                for i in range(2):
                    g = 2 * half + i
                    hi = act.activation(qt[:, b, 0, g, :], B4[:, i * TA:(i + 1) * TA], ACT.Identity,
                                        bias=bqs_c[:, g:g + 1])
                hi.then_inc(q_hi, 1)

            act.wait_ge(in_wq, 16)
            act.activation(wq_r[:, 0, :, :], wq_f, ACT.Copy, scale=SCALE).then_inc(wq_hi, 1)
            turned_z(0, 0)
            act.wait_ge(bqs_ready, 1)
            q_high(0, 0, 0)
            q_high(0, 0, 1)
            act.wait_ge(v_copied, 2)
            act.dma_start(bias_row[:, :], bo.partition_broadcast(P)).then_inc(in_bo, 16)
            act.wait_ge(in_wo, 16)
            act.activation(wo_r[:, 0, :, :], wo_f, ACT.Copy).then_inc(wo_hi, 1)
            turned_z(0, 1)
            act.wait_ge(v_placed, 16 * N_PIECES)
            for b in range(B):
                hi = act.activation(vblk[:, b, 0, :, :], vpl_f[:, b, :, :], ACT.Copy)
            hi.then_inc(vb_hi, 1)

            def probs_high(j, b, u, parts):
                s = 2 * (2 * j + b) + u
                for part in parts:
                    c0, bk_ = 4 * part, (B5, B6, B5)[part]
                    nch = min(4, NCH - c0)
                    act.wait_ge(pt_full, 3 * s + (part + 1))
                    act.activation(pt[:, 0, c0:c0 + nch, u * P:(u + 1) * P],
                                   bk_[:, 0:nch * P].rearrange("p (c t) -> p c t", c=nch),
                                   ACT.Copy).then_inc(pt_hi, 1)

            def exponent(j, b, u):
                k = 2 * b + u
                act.wait_ge(s_sub, 2 * num(j, b) + u + 1)
                act.activation(sc[:, k, 0:HKV], sc[:, k, 0:HKV], ACT.Exp).then_inc(s_exp, 1)

            def heads_high(j, b):
                n = 2 * j + b
                for half, bk_ in ((0, B5), (1, B6)):
                    act.wait_ge(pv_full, 2 * n + half + 1)
                    act.activation(ot[:, 0, 2 * half:2 * half + 2, :],
                                   bk_[:, :].rearrange("p (g t) -> p g t", g=2), ACT.Copy).then_inc(ot_hi, 1)

            def body(j):
                for b in range(2):
                    before, after = there(NA, j, b, -1), there(NA, j, b, 1)
                    for u in range(2):
                        if before:
                            probs_high(*shift(j, b, -1), u, (0, 1))
                        if after:
                            q_high(*shift(j, b, 1), u)
                        if before:
                            probs_high(*shift(j, b, -1), u, (2,))
                        if u == 0 and there(NA, j, b, 0):
                            exponent(j, b, 0)
                    if there(NA, j, b, 2):
                        turned_z(j + 1, b)
                    if there(NA, j, b, 0):
                        exponent(j, b, 1)
                    if before:
                        heads_high(*shift(j, b, -1))

            pairs(act, NA, body)

            act.wait_ge(o_full, 2 * NA)
            act.wait_ge(in_ffn, 4 * 16)
            act.activation(u1_r[:, 0, :, :], u1_f, ACT.Copy).then_inc(ffn_hi, 1)
            act.activation(v1_r[:, 0, :], v1_f, ACT.Copy).then_inc(ffn_hi, 1)
            act.activation(u2_r[:, 0, :, :], u2_f, ACT.Copy).then_inc(ffn_hi, 1)
            act.activation(v2_r[:, 0, :], v2_f, ACT.Copy).then_inc(ffn_hi, 1)
            act.wait_ge(xb_done, 2 * NA)
            act.dma_start(bias_row[:, :], b2.partition_broadcast(P)).then_inc(in_b2, 16)

            def turned_z2(j, b, t):
                act.wait_ge(z2t_full, UB * (2 * j + b) + t + 1)
                act.activation(z2t[:, 0, :, t * P:(t + 1) * P],
                               (B6, B7)[t % 2][:, :].rearrange("p (k t) -> p k t", k=KD),
                               ACT.Copy).then_inc(z2t_hi, 1)

            def p1_high(j, b):
                act.wait_ge(p1_full, 2 * j + b + 1)
                act.activation(p1t[:, b, 0, :], B6[:, :], ACT.Copy).then_inc(p1_hi, 1)

            def q2_high(j, b):
                act.wait_ge(u2_done, NFF * (2 * j + b + 1))
                act.activation(q2t[:, 0, :], (B4, B5)[b][:, :], ACT.Copy).then_inc(q2_hi, 1)

            for t in range(UB):
                turned_z2(0, 0, t)
            p1_high(0, 0)

            def body2(j):
                for b in range(2):
                    for c in range(NFF):
                        if there(NB, j, b, 0):
                            n = NFF * num(j, b) + c
                            act.wait_ge(h_full, n + 1)
                            if not isinstance(j, int) or n >= 4:
                                if c % 2:
                                    act.wait_ge(h_lo_pool, 8 * num(j, b) + (c + 1) // 2 - 2)
                                else:
                                    act.wait_ge(h_lo, 8 * num(j, b) + c // 2 - 1)
                            act.activation(hg[:, c % 4, :], ps_s[:, c % 4, :], ACT.Gelu_apprx_tanh,
                                           bias=b1_c[:, c:c + 1]).then_inc(h_gelu, 1)
                        if c == 3 and there(NB, j, b, -1):
                            q2_high(*shift(j, b, -1))
                        if c in (5, 6, 7, 8) and there(NB, j, b, 1):
                            turned_z2(*shift(j, b, 1), c - 5)
                        if c == 13 and there(NB, j, b, 1):
                            p1_high(*shift(j, b, 1))

            pairs(act, NB, body2)

        @block.vector
        def _(dve):
            def norm_stats(j, b, u):
                k = 2 * b + u
                n = 2 * (2 * j + b) + u
                dve.wait_ge(in_x[k], 16 * (j + 1))
                until(dve, z_done, n - 3)
                dve.bn_stats(stats[:, k, :], xa[:, k, :]).then_inc(stats_done, 1)
                dve.wait_ge(stats_done, n + 1)
                dve.memset(stall[:, :], 0.0)
                dve.bn_aggr(mv[:, k, :], stats[:, k, :]).then_inc(mv_done, 1)

            def norm_z(j, b):
                n = 2 * j + b
                dve.wait_ge(rstd_done, n + 1)
                for u in range(2):
                    k = 2 * b + u
                    until(dve, zt_full, 2 * n + u - 1)
                    dve.tensor_scalar(z[:, u, :], xa[:, k, :], mv[:, k, 0:1], rstd[:, k:k + 1],
                                      ALU.subtract, ALU.mult).then_inc(z_done, 1)

            def turned_z(j, b):
                n = 2 * j + b
                for u, bk_ in ((0, B6), (1, B4)):
                    dve.wait_ge(zt_hi, 2 * n + u + 1)
                    dve.tensor_tensor(zt[:, 1, :, u * P:(u + 1) * P],
                                      bk_[:, :].rearrange("p (k t) -> p k t", k=KD),
                                      zt[:, 0, :, u * P:(u + 1) * P].bitcast(F32),
                                      ALU.subtract).then_inc(zt_lo, 1)

            def q_low(j, b, half):
                n = 2 * j + b
                dve.wait_ge(q_hi, 2 * n + half + 1)
                for i in range(2):
                    g = 2 * half + i
                    lo = dve.scalar_tensor_tensor(qt[:, b, 1, g, :], B4[:, i * TA:(i + 1) * TA],
                                                  bqs_c[:, g:g + 1], qt[:, b, 0, g, :].bitcast(F32),
                                                  ALU.add, ALU.subtract)
                lo.then_inc(q_lo, 1)

            norm_stats(0, 0, 0)
            norm_stats(0, 0, 1)
            norm_z(0, 0)
            dve.wait_ge(bias_turned, 1)
            dve.tensor_scalar(bqs_c[:, :], B5[:, 0:G], SCALE, None, ALU.mult)
            dve.tensor_copy(bk_c[:, :], B5[:, G:2 * G])
            dve.tensor_copy(b1_c[:, :], B5[:, 2 * G:2 * G + NFF]).then_inc(bqs_ready, 1)
            dve.wait_ge(wq_hi, 1)
            dve.scalar_tensor_tensor(wq_r[:, 1, :, :].rearrange("p k n -> p (k n)"),
                                     wq_f.rearrange("p k n -> p (k n)"), SCALE,
                                     wq_r[:, 0, :, :].rearrange("p k n -> p (k n)").bitcast(F32),
                                     ALU.mult, ALU.subtract).then_inc(wq_lo, 1)
            turned_z(0, 0)
            norm_stats(0, 1, 0)
            norm_stats(0, 1, 1)
            norm_z(0, 1)
            dve.wait_ge(bqs_ready, 1)
            q_low(0, 0, 0)
            q_low(0, 0, 1)
            dve.wait_ge(ctx_turned, 1)
            dve.tensor_copy(ctxt_f[:, :, :, :].rearrange("p k b w -> p (k b w)"),
                            B7[:, 0:KC * B * KV]).then_inc(ctx_copied, 1)
            dve.wait_ge(k_full, 1)
            dve.wait_ge(bqs_ready, 1)
            for g in range(G):
                src = (B5 if g < 3 else B6)[:, (g % 3) * B * KV:(g % 3 + 1) * B * KV]
                last = dve.tensor_scalar(kt_f[:, g, :, :].rearrange("p b w -> p (b w)"), src,
                                         bk_c[:, g:g + 1], None, ALU.add)
            last.then_inc(k_copied, 1)
            dve.wait_ge(k_copied, 1)
            dve.wait_ge(zeroed, 1)
            for part in range(2):
                for i in range(GH):
                    p0 = i * DH
                    src = kt_f[p0:p0 + DH, :, :, :].rearrange("p g b w -> p b g w")
                    hi = kblk[p0:p0 + DH, :, 0, :, i * KV:(i + 1) * KV]
                    lo = kblk[p0:p0 + DH, :, 1, :, i * KV:(i + 1) * KV]
                    for b in range(B):
                        if part == 0:
                            last = dve.tensor_copy(hi[:, b], src[:, b])
                        else:
                            last = dve.tensor_tensor(lo[:, b], src[:, b], hi[:, b].bitcast(F32), ALU.subtract)
                last.then_inc((kb_hi, kb_lo)[part], 1)
                dve.wait_ge((kb_hi, kb_lo)[part], 1)
            dve.wait_ge(in_bv, 16)
            for b in range(B):
                dve.wait_ge(v_full, b + 1)
                dve.tensor_tensor(v_f[:, b, :], (B7[0:KV, :], ps_s[0:KV, 0, :])[b], bias_row[0:KV, :],
                                  ALU.add).then_inc(v_copied, 1)
            for k in range(4):
                last = dve.memset(sc[:, k, HKV:], 0.0)
            last.then_inc(pad_zero, 1)
            turned_z(0, 1)
            norm_stats(1, 0, 0)
            norm_stats(1, 0, 1)
            dve.wait_ge(wo_hi, 1)
            dve.tensor_tensor(wo_r[:, 1, :, :], wo_f, wo_r[:, 0, :, :].bitcast(F32),
                              ALU.subtract).then_inc(wo_lo, 1)
            dve.wait_ge(vb_hi, 1)
            for b in range(B):
                last = dve.tensor_tensor(vblk[:, b, 1, :, :], vpl_f[:, b, :, :],
                                         vblk[:, b, 0, :, :].bitcast(F32), ALU.subtract)
            last.then_inc(vb_lo, 1)

            def clip(j, b, u):
                k, s = 2 * b + u, 2 * (2 * j + b) + u
                dve.wait_ge(s_full, s + 1)
                until(dve, pt_full, 3 * (s - 3))
                dve.tensor_scalar(sc[:, k, 0:HKV].rearrange("p (g w) -> p g w", g=G), ps_s[:, :, 0:GW],
                                  CLAMP, -CLAMP, ALU.min, ALU.max).then_inc(s_clip, 1)

            def heads(k):
                return sc[:, k, 0:HKV].rearrange("p (h w) -> p h w", h=H)

            def maxima(j, b, u):
                k, s = 2 * b + u, 2 * (2 * j + b) + u
                dve.wait_ge(s_clip, s + 1)
                dve.tensor_reduce(smax[:, k, :], heads(k), AX.X, ALU.max).then_inc(s_max, 1)

            def sums(j, b, u):
                k, s = 2 * b + u, 2 * (2 * j + b) + u
                dve.wait_ge(s_exp, s + 1)
                dve.tensor_reduce(ssum[:, k, :], heads(k), AX.X, ALU.add).then_inc(s_sum, 1)
                dve.wait_ge(s_sum, s + 1)
                dve.reciprocal(rsum[:, k, :], ssum[:, k, :]).then_inc(s_rec, 1)

            def probs_low(j, b, u, parts):
                s = 2 * (2 * j + b) + u
                for part in parts:
                    c0, bk_ = 4 * part, (B5, B6, B5)[part]
                    nch = min(4, NCH - c0)
                    dve.wait_ge(pt_hi, 3 * s + (part + 1))
                    dve.tensor_tensor(pt[:, 1, c0:c0 + nch, u * P:(u + 1) * P],
                                      bk_[:, 0:nch * P].rearrange("p (c t) -> p c t", c=nch),
                                      pt[:, 0, c0:c0 + nch, u * P:(u + 1) * P].bitcast(F32),
                                      ALU.subtract).then_inc(pt_lo, 1)

            def heads_low(j, b):
                n = 2 * j + b
                for half, bk_ in ((0, B5), (1, B6)):
                    dve.wait_ge(ot_hi, 2 * n + half + 1)
                    dve.tensor_tensor(ot[:, 1, 2 * half:2 * half + 2, :],
                                      bk_[:, :].rearrange("p (g t) -> p g t", g=2),
                                      ot[:, 0, 2 * half:2 * half + 2, :].bitcast(F32),
                                      ALU.subtract).then_inc(ot_lo, 1)

            def y_sum(j, b, u):
                k, s = 2 * b + u, 2 * (2 * j + b) + u
                dve.wait_ge(o_full, s + 1)
                dve.wait_ge(xb_done, s + 1)
                dve.tensor_tensor(xb[:, k, :], B7[:, :], xb[:, k, :], ALU.add).then_inc(y_done, 1)

            def body(j):
                for b in range(2):
                    here, before, after = there(NA, j, b, 0), there(NA, j, b, -1), there(NA, j, b, 1)
                    for u in range(2):
                        if here:
                            clip(j, b, u)
                        if before:
                            probs_low(*shift(j, b, -1), u, (0,))
                        if here:
                            maxima(j, b, u)
                        if before:
                            probs_low(*shift(j, b, -1), u, (1,))
                        if u == 1 and here:
                            sums(j, b, 0)
                        if after:
                            q_low(*shift(j, b, 1), u)
                        if before:
                            probs_low(*shift(j, b, -1), u, (2,))
                        if u == 0 and there(NA, j, b, 2):
                            norm_z(j + 1, b)
                        if there(NA, j, b, -2):
                            y_sum(j - 1, b, u)
                        if there(NA, j, b, 3):
                            norm_stats(*shift(j, b, 3), u)
                    if there(NA, j, b, 2):
                        turned_z(j + 1, b)
                    if here:
                        sums(j, b, 1)
                    if before:
                        heads_low(*shift(j, b, -1))

            pairs(dve, NA, body)

            for i, (lo, src, hi) in enumerate((
                    (u1_r[:, 1, :, :], u1_f, u1_r[:, 0, :, :]), (v1_r[:, 1, :], v1_f, v1_r[:, 0, :]),
                    (u2_r[:, 1, :, :], u2_f, u2_r[:, 0, :, :]), (v2_r[:, 1, :], v2_f, v2_r[:, 0, :]))):
                dve.wait_ge(ffn_hi, i + 1)
                dve.tensor_tensor(lo, src, hi.bitcast(F32), ALU.subtract).then_inc(ffn_lo, 1)

            def norm_stats2(j, b, t):
                n = UB * (2 * j + b) + t
                dve.wait_ge(in_y[b], 16 * (j + 1))
                dve.bn_stats(stats[:, t, :], ya[:, b, t, :]).then_inc(stats2, 1)
                dve.wait_ge(stats2, n + 1)
                dve.memset(stall[:, :], 0.0)
                dve.bn_aggr(mv[:, t, :], stats[:, t, :]).then_inc(mv2, 1)

            def norm_z2(j, b, t):
                n = 2 * j + b
                dve.wait_ge(rstd2, n + 1)
                until(dve, z2t_full, UB * (n - 1) + t + 1)
                dve.tensor_scalar(z2[:, t, :], ya[:, b, t, :], mv[:, t, 0:1], rstd[:, t:t + 1],
                                  ALU.subtract, ALU.mult).then_inc(z2_done, 1)

            def turned_z2(j, b, t):
                dve.wait_ge(z2t_hi, UB * (2 * j + b) + t + 1)
                dve.tensor_tensor(z2t[:, 1, :, t * P:(t + 1) * P],
                                  (B6, B7)[t % 2][:, :].rearrange("p (k t) -> p k t", k=KD),
                                  z2t[:, 0, :, t * P:(t + 1) * P].bitcast(F32),
                                  ALU.subtract).then_inc(z2t_lo, 1)

            def p1_low(j, b):
                dve.wait_ge(p1_hi, 2 * j + b + 1)
                dve.tensor_tensor(p1t[:, b, 1, :], B6[:, :], p1t[:, b, 0, :].bitcast(F32),
                                  ALU.subtract).then_inc(p1_lo, 1)

            def q2_low(j, b):
                dve.wait_ge(q2_hi, 2 * j + b + 1)
                dve.tensor_tensor(q2t[:, 1, :], (B4, B5)[b][:, :], q2t[:, 0, :].bitcast(F32),
                                  ALU.subtract).then_inc(q2_lo, 1)

            def out_sum(j, b, t):
                n = UB * (2 * j + b) + t
                dve.wait_ge(o2_full, n + 1)
                dve.wait_ge(yb_done, n + 1)
                dve.tensor_tensor(yb[:, b, t, :], (B6, B7)[t % 2][:, :], yb[:, b, t, :],
                                  ALU.add).then_inc(o2_done, 1)

            for t in range(UB):
                norm_stats2(0, 0, t)
            for t in range(UB):
                norm_z2(0, 0, t)
            for t in range(UB):
                turned_z2(0, 0, t)
            for t in range(UB):
                norm_stats2(0, 1, t)
            for t in range(UB):
                norm_z2(0, 1, t)
            p1_low(0, 0)

            def body2(j):
                for b in range(2):
                    for c in range(NFF):
                        if there(NB, j, b, 0):
                            n = NFF * num(j, b) + c
                            dve.wait_ge(h_gelu, n + 1)
                            if not isinstance(j, int) or n >= 4:
                                dve.wait_ge(u2_done, n - 3)
                            dve.tensor_copy(hs[:, c % 4, 0, :], hg[:, c % 4, :]).then_inc(h_hi, 1)
                            if c % 2 == 0:
                                dve.wait_ge(h_hi, n + 1)
                                dve.tensor_tensor(hs[:, c % 4, 1, :], hg[:, c % 4, :],
                                                  hs[:, c % 4, 0, :].bitcast(F32), ALU.subtract)\
                                    .then_inc(h_lo, 1)
                        if c == 3 and there(NB, j, b, -1):
                            q2_low(*shift(j, b, -1))
                        if c in (5, 6, 7, 8) and there(NB, j, b, 1):
                            turned_z2(*shift(j, b, 1), c - 5)
                        if c in (7, 8, 9, 10) and there(NB, j, b, 2):
                            norm_stats2(j + 1, b, c - 7)
                        if c in (9, 10, 11, 12) and there(NB, j, b, -1):
                            out_sum(*shift(j, b, -1), c - 9)
                        if c in (12, 13, 14, 15) and there(NB, j, b, 2):
                            norm_z2(j + 1, b, c - 12)
                        if c == 13 and there(NB, j, b, 1):
                            p1_low(*shift(j, b, 1))

            pairs(dve, NB, body2)

        @block.tensor
        def _(pe):
            def product(ps, lhs, rhs, first=True, last=True):
                for i, (a, c) in enumerate(PASSES):
                    mm = pe.matmul(ps, lhs(a), rhs(c), start=first and i == 0,
                                   stop=last and i == len(PASSES) - 1)
                return mm

            def turn_z(j, b):
                n = 2 * j + b
                for u, bk_ in ((0, B6), (1, B4)):
                    pe.wait_ge(z_done, 2 * n + u + 1)
                    if u == 0:
                        if isinstance(j, int) and n < 3:
                            until(pe, zt_lo, 2 * n - 1)
                        else:
                            pe.wait_ge(pt_lo, 6 * n - 13)
                    else:
                        until(pe, q_lo, 2 * n)
                    for k in range(KD):
                        last = pe.transpose(bk_[:, k * P:(k + 1) * P], z[:, u, k * P:(k + 1) * P],
                                            ident[:, :])
                    last.then_inc(zt_full, 1)

            def project_q(j, b, half):
                n = 2 * j + b
                pe.wait_ge(zt_lo, 2 * n + 2)
                if half:
                    pe.wait_ge(q_lo, 2 * n + 1)
                for i in range(2):
                    g = 2 * half + i
                    for k in range(KD):
                        last = product(B4[:, i * TA:(i + 1) * TA],
                                       lambda a: wq_r[:, a, k, g * P:(g + 1) * P],
                                       lambda a: zt[:, a, k, :], k == 0, k == KD - 1)
                last.then_inc(q_full, 1)

            def scores(j, b, u):
                n = 2 * j + b
                pe.wait_ge(q_lo, 2 * n + 2)
                until(pe, s_clip, 2 * n + u)
                for g in range(G):
                    last = product(ps_s[:, g, 0:GW], lambda a: qt[:, b, a, g, u * P:(u + 1) * P],
                                   lambda a: kblk[:, b, a, g, :])
                last.then_inc(s_full, 1)

            def turn_probs(j, b, u, parts):
                k, n = 2 * b + u, 2 * j + b
                s = 2 * n + u
                for part in parts:
                    bk_ = (B5, B6, B5)[part]
                    if part == 0:
                        pe.wait_ge(s_norm, s + 1)
                        if u == 0:
                            until(pe, ot_lo, 2 * n - 1)
                        else:
                            pe.wait_ge(pt_lo, 3 * s)
                    elif part == 1 and u == 0:
                        if isinstance(j, int) and n == 0:
                            pe.wait_ge(zt_lo, 5)
                        else:
                            pe.wait_ge(ot_lo, 2 * n)
                    elif part == 2:
                        pe.wait_ge(pt_lo, 3 * s + 1)
                    for c in range(4 * part, min(4 * part + 4, NCH)):
                        last = pe.transpose(bk_[:, (c % 4) * P:(c % 4 + 1) * P],
                                            sc[:, k, c * P:(c + 1) * P], ident[:, :])
                    last.then_inc(pt_full, 1)

            def weigh_values(j, b):
                n = 2 * j + b
                pe.wait_ge(pt_lo, 6 * n + 6)
                if not isinstance(j, int) or n + 3 < NA:
                    pe.wait_ge(zt_lo, 2 * (n + 3) + 1)
                for half, bk_ in ((0, B5), (1, B6)):
                    for i in range(2):
                        g = 2 * half + i
                        mine = [(q, c) for q, (c, gg) in enumerate(PAIRS) if gg == g]
                        for q, c in mine:
                            last = product(bk_[:, i * TA:(i + 1) * TA], lambda a: vblk[:, b, a, q, :],
                                           lambda a: pt[:, a, c, :], q == mine[0][0], q == mine[-1][0])
                    last.then_inc(pv_full, 1)

            def project_out(j, b, u):
                n = 2 * j + b
                pe.wait_ge(ot_lo, 2 * n + 2)
                until(pe, y_done, 2 * n + u)
                for k in range(KD):
                    last = product(B7[:, :], lambda a: ot[:, a, k, u * P:(u + 1) * P],
                                   lambda a: wo_r[:, a, k, :], k == 0, k == KD - 1)
                last.then_inc(o_full, 1)

            pe.wait_ge(const_ready, 4)
            pe.wait_ge(in_bias, 3 * 16)
            pe.transpose(B5[:, 0:2 * G + NFF], bias_f[:, :], ident[0:2 * G + NFF, 0:2 * G + NFF])\
              .then_inc(bias_turned, 1)
            turn_z(0, 0)
            pe.wait_ge(wq_lo, 1)
            project_q(0, 0, 0)
            project_q(0, 0, 1)
            pe.wait_ge(in_ctx, 16)
            for k in range(KC):
                for b in range(B):
                    o = (k * B + b) * KV
                    last = pe.transpose(B7[:, o:o + KV], ctx_f[:, b, k * P:(k + 1) * P], ident[0:KV, 0:KV])
            last.then_inc(ctx_turned, 1)
            turn_z_1 = lambda: turn_z(0, 1)
            pe.wait_ge(ctx_copied, 1)
            pe.wait_ge(in_wk, 16)
            pe.wait_ge(zt_lo, 1)
            pe.wait_ge(bqs_ready, 1)
            for g in range(G):
                dst = (B5 if g < 3 else B6)[:, (g % 3) * B * KV:(g % 3 + 1) * B * KV]
                for k in range(KC):
                    last = pe.matmul(dst, wk_f[:, k, g * P:(g + 1) * P],
                                     ctxt_f[:, k, :, :].rearrange("p b w -> p (b w)"),
                                     start=k == 0, stop=k == KC - 1)
            last.then_inc(k_full, 1)
            pe.wait_ge(in_wv, 16)
            for b in range(B):
                dst = (B7[0:KV, :], ps_s[0:KV, 0, :])[b]
                for k in range(KC):
                    last = pe.matmul(dst, ctxt_f[:, k, b, :], wv_f[:, k, :], start=k == 0, stop=k == KC - 1)
                last.then_inc(v_full, 1)
            pe.wait_ge(k_copied, 1)
            turn_z_1()
            pe.wait_ge(kb_lo, 1)
            pe.wait_ge(v_copied, 2)

            def body(j):
                for b in range(2):
                    here, before, after = there(NA, j, b, 0), there(NA, j, b, -1), there(NA, j, b, 1)
                    for u in range(2):
                        if here:
                            scores(j, b, u)
                        if before:
                            if isinstance(j, int) and num(j, b, -1) == 0 and u == 0:
                                pe.wait_ge(pad_zero, 1)
                            turn_probs(*shift(j, b, -1), u, (0, 1))
                        if after:
                            project_q(*shift(j, b, 1), u)
                        if before:
                            turn_probs(*shift(j, b, -1), u, (2,))
                        if there(NA, j, b, -2):
                            if isinstance(j, int) and num(j, b, -2) == 0 and u == 0:
                                pe.wait_ge(wo_lo, 1)
                            project_out(j - 1, b, u)
                    if there(NA, j, b, 2):
                        turn_z(j + 1, b)
                    if before:
                        if isinstance(j, int) and num(j, b, -1) == 0:
                            pe.wait_ge(vb_lo, 1)
                        weigh_values(*shift(j, b, -1))

            pairs(pe, NA, body)

            def turn_z2(j, b, t):
                n = 2 * j + b
                bk_ = (B6, B7)[t % 2]
                pe.wait_ge(z2_done, UB * n + t + 1)
                if t == 0:
                    until(pe, p1_lo, n)
                elif t == 1:
                    until(pe, o2_done, UB * (n - 2))
                else:
                    pe.wait_ge(z2t_lo, UB * n + t - 1)
                for k in range(KD):
                    last = pe.transpose(bk_[:, k * P:(k + 1) * P], z2[:, t, k * P:(k + 1) * P], ident[:, :])
                last.then_inc(z2t_full, 1)

            def project_u1(j, b):
                n = 2 * j + b
                pe.wait_ge(z2t_lo, UB * (n + 1))
                until(pe, o2_done, UB * (n - 2) + 3)
                for k in range(KD):
                    last = product(B6[:, :], lambda a: u1_r[:, a, k, :], lambda a: z2t[:, a, k, :],
                                   k == 0, k == KD - 1)
                last.then_inc(p1_full, 1)

            def hidden(j, b, c):
                n = 2 * j + b
                if c == 0:
                    pe.wait_ge(p1_lo, n + 1)
                if not isinstance(j, int) or NFF * n + c >= 4:
                    pe.wait_ge(h_gelu, NFF * n + c - 3)
                product(ps_s[:, c % 4, :], lambda a: v1_r[:, a, c * P:(c + 1) * P],
                        lambda a: p1t[:, b, a, :]).then_inc(h_full, 1)

            def project_u2(j, b, c):
                n = 2 * j + b
                if c % 2:
                    pe.wait_ge(h_lo_pool, 8 * n + (c + 1) // 2)
                else:
                    pe.wait_ge(h_lo, 8 * n + c // 2 + 1)
                if c == 0:
                    until(pe, q2_lo, n - 1)
                product((B4, B5)[b][:, :], lambda a: u2_r[:, a, c, :], lambda a: hs[:, c % 4, a, :],
                        c == 0, c == NFF - 1).then_inc(u2_done, 1)

            def project_v2(j, b, t):
                n = 2 * j + b
                if t == 0:
                    pe.wait_ge(q2_lo, n + 1)
                if t < 2:
                    if not isinstance(j, int) or n + 2 < NB:
                        pe.wait_ge(z2t_lo, UB * (n + 2) + t + 3)
                    else:
                        until(pe, o2_done, UB * n + t - 2)
                else:
                    pe.wait_ge(o2_done, UB * n + t - 1)
                product((B6, B7)[t % 2][:, :], lambda a: q2t[:, a, t * P:(t + 1) * P],
                        lambda a: v2_r[:, a, :]).then_inc(o2_full, 1)

            pe.wait_ge(y_done, 2 * NA)
            for t in range(UB):
                turn_z2(0, 0, t)
            pe.wait_ge(ffn_lo, 4)
            project_u1(0, 0)

            def body2(j):
                for b in range(2):
                    for c in range(NFF):
                        if there(NB, j, b, 0):
                            hidden(j, b, c)
                        if c >= 3 and there(NB, j, b, 0):
                            project_u2(j, b, c - 3)
                        if c < 3 and there(NB, j, b, -1):
                            project_u2(*shift(j, b, -1), NFF + c - 3)
                        if c in (4, 5, 6, 7) and there(NB, j, b, 1):
                            turn_z2(*shift(j, b, 1), c - 4)
                        if c in (8, 9, 10, 11) and there(NB, j, b, -1):
                            project_v2(*shift(j, b, -1), c - 8)
                        if c == 12 and there(NB, j, b, 1):
                            project_u1(*shift(j, b, 1))

            pairs(pe, NB, body2)


_NAMES = ["x", "ctx_768", "L0_xattn_Wq", "L0_xattn_bq", "L0_xattn_Wk", "L0_xattn_bk", "L0_xattn_Wv",
          "L0_xattn_bv", "L0_xattn_Wo", "L0_xattn_bo", "L0_ffn_U1", "L0_ffn_V1", "L0_ffn_b1",
          "L0_ffn_U2", "L0_ffn_V2", "L0_ffn_b2"]


def kernel(**inputs):
    import numpy as np
    import concourse.bacc as bacc
    from concourse.bass_utils import run_bass_kernel_spmd

    nc = bacc.Bacc("TRN2", target_bir_lowering=False, num_devices=1)
    arrays, args = {}, []
    for name in _NAMES:
        a = np.ascontiguousarray(inputs[name])
        arrays[f"in_{name}"] = a
        args.append(nc.dram_tensor(f"in_{name}", a.shape, mybir.dt.from_np(a.dtype), kind="ExternalInput").ap())
    out = nc.dram_tensor("out", inputs["x"].shape, F32, kind="ExternalOutput").ap()
    xattn_ffn(nc, *args, out)
    r = run_bass_kernel_spmd(nc, [arrays], core_ids=[0])
    return r.results[0]["out"]
```

```python
import concourse.bass as bass
from concourse import mybir
from contextlib import ExitStack

F32 = mybir.dt.float32
F32R = mybir.dt.float32r
ALU = mybir.AluOpType
ACT = mybir.ActivationFunctionType
AX = mybir.AxisListType

P = 128
B, S, D = 2, 2048, 512
KV, CKV = 77, 384
H = 16
DH = D // H
GH = P // DH
G = H // GH
GW = GH * KV
HKV = H * KV
NCH = -(-HKV // P)
KD = D // P
KC = CKV // P
R, FF = 128, 2048
NFF = FF // P
EPS = 1e-5
CLAMP = 10000.0
SCALE = DH ** -0.5
PAIRS = [(c, g) for g in range(G) for c in range(NCH) if c * P < (g + 1) * GW and (c + 1) * P > g * GW]
NP = len(PAIRS)

TA = 256
NA = B * S // TA
TPB = S // P
TB = 512
UB = TB // P
NB = B * S // TB


def num(j, b, d=0):
    return 2 * j + (b + d)


def there(total, j, b, d):
    return not isinstance(j, int) or 0 <= 2 * j + b + d < total


def shift(j, b, d):
    return j + (b + d) // 2, (b + d) % 2


def is_block(n, j, b):
    return isinstance(j, int) and 2 * j + b == n


def until(eng, sem, value):
    if not isinstance(value, int) or value > 0:
        eng.wait_ge(sem, value)


def pairs(eng, total, body):
    head = 2 if total > 8 else 1
    for j in range(head):
        body(j)
    with eng.Fori(head, total // 2 - 1) as j:
        body(j)
    body(total // 2 - 1)
    body(total // 2)


def xattn_ffn(nc, x, ctx, wq, bq, wk, bk, wv, bv, wo, bo, u1, v1, b1, u2, v2, b2, out):
    x_t = x.rearrange("b (t p) d -> (b t) p d", p=P)
    y_dram = nc.dram_tensor("y_between", [B * S, D], F32).ap()
    y_t = y_dram.rearrange("(t p) d -> t p d", p=P)
    y_b = y_dram.rearrange("(n t p) d -> n p t d", p=P, t=UB)
    out_t = out.rearrange("b (t p) d -> (b t) p d", p=P)

    stack = ExitStack()
    with stack:
        def sb(name, shape, dt=F32):
            return stack.enter_context(nc.sbuf_tensor(name, shape, dt))

        def sem(name):
            return stack.enter_context(nc.semaphore(name))

        wqo_r = sb("wqo_r", [P, 2 * 2 * KD * D], F32R)
        wq_r = wqo_r[:, 0:2 * KD * D].rearrange("p (h k n) -> p h k n", h=2, k=KD)
        wo_r = wqo_r[:, 2 * KD * D:].rearrange("p (h k n) -> p h k n", h=2, k=KD)
        kb_t = sb("kblk_r", [P, B * 2 * G * GW], F32R)
        kblk = kb_t[:, :].rearrange("p (b h g w) -> p b h g w", b=B, h=2, g=G)
        vb_t = sb("vblk_r", [P, B * 2 * NP * P], F32R)
        vblk = vb_t[:, :].rearrange("p (b h c n) -> p b h c n", b=B, h=2, c=NP)
        zt_t = sb("zt_r", [P, 2 * KD * TA], F32R)
        zt = zt_t[:, :].rearrange("p (h k t) -> p h k t", h=2, k=KD)
        qt_t = sb("qt_r", [P, 2 * 2 * G * TA], F32R)
        qt = qt_t[:, :].rearrange("p (b h g t) -> p b h g t", b=2, h=2, g=G)
        ot = sb("ot_r", [P, 2, G, TA], F32R)
        pt_t = sb("pt_r", [P, 2 * NCH * TA], F32R)
        pt = pt_t[:, :].rearrange("p (h c t) -> p h c t", h=2, c=NCH)
        z2t = wqo_r[:, 0:2 * KD * TB].rearrange("p (h k t) -> p h k t", h=2, k=KD)
        u1_r = zt_t[:, 0:2 * KD * R].rearrange("p (h k n) -> p h k n", h=2, k=KD)
        v2_r = zt_t[:, 2 * KD * R:2 * KD * R + 2 * D].rearrange("p (h n) -> p h n", h=2)
        v1_r = kb_t[:, 0:2 * FF].rearrange("p (h n) -> p h n", h=2)
        p1t = qt_t[:, 0:4 * TB].rearrange("p (b h t) -> p b h t", b=2, h=2)
        q2t = qt_t[:, 4 * TB:6 * TB].rearrange("p (h t) -> p h t", h=2)
        u2_r = vb_t[:, 0:2 * NFF * R].rearrange("p (h k n) -> p h k n", h=2, k=NFF)
        hs = pt_t[:, 0:8 * TB].rearrange("p (s h t) -> p s h t", s=4, h=2)

        xs = sb("xs", [P, 8 * D])
        xa = xs[:, 0:4 * D].rearrange("p (s d) -> p s d", s=4)
        xb = xs[:, 4 * D:].rearrange("p (s d) -> p s d", s=4)
        ss = sb("ss", [P, 4 * NCH * P])
        sc = ss[:, :].rearrange("p (s w) -> p s w", s=4)
        hg = ss[:, 0:4 * TB].rearrange("p (s t) -> p s t", s=4)
        fw = sb("fw", [P, 2 * FF + KD * R + D])
        z = sb("z", [P, 2, D])
        wq_f = ss[:, 0:KD * D].rearrange("p (k n) -> p k n", k=KD)
        wv_f = ss[:, KD * D:KD * D + KC * D].rearrange("p (k n) -> p k n", k=KC)
        ctx_f = ss[0:KV, (KD + KC) * D:(KD + KC) * D + B * CKV].rearrange("p (b c) -> p b c", b=B)
        wo_f = xb
        vpl_f = fw[:, 0:B * NP * P].rearrange("p (b c n) -> p b c n", b=B, c=NP)
        wk_f = fw[:, B * NP * P:B * NP * P + KC * D].rearrange("p (k n) -> p k n", k=KC)
        once = sb("once", [P, KC * B * KV + G * B * KV + B * D])
        ctxt_f = once[:, 0:KC * B * KV].rearrange("p (k b w) -> p k b w", k=KC, b=B)
        kt_f = once[:, KC * B * KV:(KC + G) * B * KV].rearrange("p (g b w) -> p g b w", g=G, b=B)
        v_f = once[0:KV, (KC + G) * B * KV:].rearrange("p (b d) -> p b d", b=B)
        z2 = once[:, 0:UB * D].rearrange("p (t d) -> p t d", t=UB)
        v1_f = fw[:, 0:FF]
        u2_f = fw[:, FF:2 * FF].rearrange("p (k n) -> p k n", k=NFF)
        u1_f = fw[:, 2 * FF:2 * FF + KD * R].rearrange("p (k n) -> p k n", k=KD)
        v2_f = fw[:, 2 * FF + KD * R:]
        ya = [xa, fw[:, 0:UB * D].rearrange("p (t d) -> p t d", t=UB)]
        yb = [fw[:, FF:FF + UB * D].rearrange("p (t d) -> p t d", t=UB), xb]
        bias_row = sb("bias_row", [P, D])
        bias_f = sb("bias_f", [2 * G + NFF, P])
        bqs_c = sb("bqs_c", [P, G])
        bk_c = sb("bk_c", [P, G])
        b1_c = sb("b1_c", [P, NFF])
        ident = sb("ident", [P, P])
        mhalf = sb("mhalf", [P, UB])
        eps_c = sb("eps_c", [P, UB])
        stall = sb("stall", [P, 1])
        stats = sb("stats", [P, 4, 6])
        stats_b, mv_b, var_b, rstd_b = (sb(n, [P, UB, w]) for n, w in (
            ("stats_b", 6), ("mv_b", 2), ("var_b", 1), ("rstd_b", 1)))
        mv = sb("mv", [P, 4, 2])
        var_e = sb("var_e", [P, 4])
        rstd = sb("rstd", [P, 4])
        smax = sb("smax", [P, 4, H])
        ssum = sb("ssum", [P, 4, H])
        rsum = sb("rsum", [P, 4, H])

        bank = [stack.enter_context(nc.psum_tensor(f"bank{i}", [P, 512], F32)) for i in range(4, 8)]
        ps_s = stack.enter_context(nc.psum_tensor("ps_s", [P, 4, 512], F32))
        B4, B5, B6, B7 = bank
        z2_bank = lambda j, b, t: (B4[:, :], ps_s[:, 0, :])[t % 2] if is_block(0, j, b) else B6[:, :]
        p1_bank = lambda j, b: B4 if is_block(0, j, b) else B6

        in_x = [sem(f"in_x{i}") for i in range(4)]
        in_xb = [sem(f"in_xb{i}") for i in range(4)]
        y_out = [sem(f"y_out{i}") for i in range(4)]
        in_wq, in_wk, in_wv, in_wo, in_ctx = (sem(n) for n in ("in_wq", "in_wk", "in_wv", "in_wo", "in_ctx"))
        in_bias, in_bv, in_bo, in_b2, bias_turned = (sem(n) for n in ("in_bias", "in_bv", "in_bo", "in_b2", "bias_turned"))
        in_ffn, v_placed = sem("in_ffn"), sem("v_placed")
        const_ready, zeroed = sem("const_ready"), sem("zeroed")
        ctx_turned, ctx_copied, k_full, v_full, k_copied, v_copied = (
            sem(n) for n in ("ctx_turned", "ctx_copied", "k_full", "v_full", "k_copied", "v_copied"))
        wq_hi, wq_lo, wo_hi, wo_lo, kb_hi, kb_lo, vb_hi, vb_lo, pad_zero, bqs_ready = (
            sem(n) for n in ("wq_hi", "wq_lo", "wo_hi", "wo_lo", "kb_hi", "kb_lo", "vb_hi", "vb_lo",
                             "pad_zero", "bqs_ready"))
        stats_done, mv_done, var_done, rstd_done, z_done = (
            sem(n) for n in ("stats_done", "mv_done", "var_done", "rstd_done", "z_done"))
        zt_full, zt_hi, zt_lo, q_full, q_hi, q_lo = (
            sem(n) for n in ("zt_full", "zt_hi", "zt_lo", "q_full", "q_hi", "q_lo"))
        s_full, s_clip, s_max, s_sub, s_exp, s_sum, s_rec, s_norm = (
            sem(n) for n in ("s_full", "s_clip", "s_max", "s_sub", "s_exp", "s_sum", "s_rec", "s_norm"))
        pt_full, pt_hi, pt_lo, pv_full, ot_hi, ot_lo, o_full, xb_done, y_done = (
            sem(n) for n in ("pt_full", "pt_hi", "pt_lo", "pv_full", "ot_hi", "ot_lo", "o_full",
                             "xb_done", "y_done"))
        ffn_hi = [sem(f"ffn_hi_{n}") for n in ("u1", "v1", "v2", "u2")]
        ffn_lo = [sem(f"ffn_lo_{n}") for n in ("u1", "v1", "v2", "u2")]
        in_y = [sem(f"in_y{i}") for i in range(2)]
        outs = [sem(f"outs{i}") for i in range(2)]
        stats2, mv2, var2, rstd2, z2_done, yb_done = (
            sem(n) for n in ("stats2", "mv2", "var2", "rstd2", "z2_done", "yb_done"))
        z2t_full, z2t_hi, z2t_lo, p1_full, p1_hi, p1_lo = (
            sem(n) for n in ("z2t_full", "z2t_hi", "z2t_lo", "p1_full", "p1_hi", "p1_lo"))
        h_full, h_gelu, h_hi, h_hi_act, h_lo, h_lo_pool, u2_done, q2_hi, q2_lo, o2_full, o2_done = (
            sem(n) for n in ("h_full", "h_gelu", "h_hi", "h_hi_act", "h_lo", "h_lo_pool", "u2_done", "q2_hi", "q2_lo",
                             "o2_full", "o2_done"))

        PASSES = ((0, 0), (0, 1), (1, 0))

        def tile_row(j, b, u):
            return 2 * j + (b * TPB + u)

        def v_pieces(h):
            r, end = h * KV, (h + 1) * KV
            while r < end:
                c = r // P
                n = min(end, (c + 1) * P) - r
                yield PAIRS.index((c, h // GH)), r % P, r - h * KV, n
                r += n

        N_PIECES = sum(len(list(v_pieces(h))) for h in range(H))

        block = stack.enter_context(nc.Block())

        def k_heads(part):
            for i in range(GH):
                p0 = i * DH
                for b in range(B):
                    yield (kblk[p0:p0 + DH, b, part, :, i * KV:(i + 1) * KV], kt_f[p0:p0 + DH, :, b, :])

        TURNS, DOWNS = (4, 6, 8, 10), (5, 7, 9, 11)

        @block.sync
        def _(sp):
            def held(value):
                return value if isinstance(value, int) else sp.snap(value)

            def load_x(j, b):
                jj, bb = j, b
                for u in range(2):
                    k = 2 * bb + u
                    row = held(tile_row(jj, bb, u))
                    until(sp, z_done, 2 * (2 * jj + bb - 2) + u + 1)
                    sp.dma_start(xa[:, k, :], x_t[row, :, :]).then_inc(in_x[k], 16)

            load_x(0, 0)
            sp.dma_start(wk_f, wk.rearrange("(k p) n -> p k n", p=P)).then_inc(in_wk, 16)
            sp.dma_start(wq_f, wq.rearrange("(k p) n -> p k n", p=P)).then_inc(in_wq, 16)
            load_x(0, 1)
            sp.dma_start(wv_f, wv.rearrange("(k p) n -> p k n", p=P)).then_inc(in_wv, 16)
            sp.dma_start(wo_f, wo.rearrange("(k p) n -> p k n", p=P)).then_inc(in_wo, 16)
            load_x(1, 0)
            sp.wait_ge(v_copied, 2)
            sp.wait_ge(zeroed, 2)
            for h in range(H):
                for c, p0, kv0, n in v_pieces(h):
                    d0 = (h % GH) * DH
                    sp.dma_start(vpl_f[p0:p0 + n, :, c, d0:d0 + DH],
                                 v_f[kv0:kv0 + n, :, h * DH:(h + 1) * DH]).then_inc(v_placed, 16)

            def load_ffn():
                sp.wait_ge(vb_lo, 1)
                sp.wait_ge(k_full, 1)
                sp.dma_start(v1_f, v1).then_inc(in_ffn, 16)
                sp.dma_start(u2_f, u2.rearrange("(k p) n -> p k n", p=P)).then_inc(in_ffn, 16)
                sp.dma_start(u1_f, u1.rearrange("(k p) n -> p k n", p=P)).then_inc(in_ffn, 16)
                sp.dma_start(v2_f, v2).then_inc(in_ffn, 16)

            def load_y(j, b):
                at, used = held(j + b * (S // TB)), held(UB * (2 * j + b - 1))
                until(sp, z2_done, used)
                until(sp, yb_done, used)
                sp.dma_start(ya[b], y_b[at, :, :, :]).then_inc(in_y[b], 16)

            def body(j):
                for b in range(2):
                    if is_block(0, j, b):
                        sp.wait_ge(wo_lo, 1)
                    if is_block(3, j, b):
                        load_ffn()
                    if there(NA, j, b, 3):
                        load_x(*shift(j, b, 3))
                    if there(NA, j, b, -2):
                        for u in range(2):
                            k = 2 * b + u
                            row = held(tile_row(j - 1, b, u))
                            sp.wait_ge(y_done, 2 * num(j, b, -2) + u + 1)
                            sp.dma_start(y_t[row, :, :], xb[:, k, :]).then_inc(y_out[k], 16)
                    if is_block(NA - 2, j, b):
                        for k in range(2):
                            sp.wait_ge(y_out[k], 16 * (TB // TA))
                        sp.wait_ge(z_done, 2 * NA)
                        load_y(0, 0)
                    if is_block(NA, j, b):
                        for k in range(2, 4):
                            sp.wait_ge(y_out[k], 16 * (TB // TA))
                        sp.wait_ge(ffn_lo[1], 1)
                        load_y(0, 1)
                    if there(NA, j, b, 0):
                        for u in range(2):
                            k = 2 * b + u
                            row = held(tile_row(j, b, u))
                            until(sp, y_out[k], 16 * j)
                            sp.dma_start(xb[:, k, :], x_t[row, :, :]).then_inc(in_xb[k], 16)

            pairs(sp, NA, body)

            for k in range(4):
                sp.wait_ge(y_out[k], 16 * (NA // 2))

            def body2(j):
                for b in range(2):
                    if there(NB, j, b, 2):
                        load_y(j + 1, b)
                    if there(NB, j, b, -1):
                        jj, bb = shift(j, b, -1)
                        for t in range(UB):
                            row = held(UB * jj + (bb * TPB + t))
                            sp.wait_ge(o2_done, UB * num(j, b, -1) + t + 1)
                            sp.dma_start(out_t[row, :, :], yb[bb][:, t, :])\
                              .then_inc(outs[bb], 16)

            pairs(sp, NB, body2)
            for b in range(2):
                sp.wait_ge(outs[b], 16 * UB * (NB // 2))

        @block.gpsimd
        def _(pool):
            pool.memset(ident[:, :], 0.0).then_inc(const_ready, 1)
            pool.memset(mhalf[:, :], -0.5).then_inc(const_ready, 1)
            pool.memset(eps_c[:, :], EPS).then_inc(const_ready, 1)
            pool.wait_ge(const_ready, 3)
            pool.affine_select(out=ident[:, :], in_=ident[:, :], compare_op=ALU.not_equal, fill=1.0,
                               base=0, pattern=[[-1, P]], channel_multiplier=1).then_inc(const_ready, 1)

            def rstd_of(j, b):
                n = 2 * j + b
                pool.wait_ge(mv_done, 2 * n + 2)
                until(pool, z_done, 2 * n - 2)
                pool.tensor_tensor(var_e[:, 2 * b:2 * b + 2], mv[:, 2 * b:2 * b + 2, 1], eps_c[:, 0:2],
                                   ALU.add).then_inc(var_done, 1)
                pool.wait_ge(var_done, n + 1)
                pool.tensor_tensor(rstd[:, 2 * b:2 * b + 2], var_e[:, 2 * b:2 * b + 2], mhalf[:, 0:2],
                                   ALU.pow).then_inc(rstd_done, 1)

            rstd_of(0, 0)
            pool.memset(kb_t[:, :].bitcast(F32), 0.0).then_inc(zeroed, 1)
            rstd_of(0, 1)
            pool.memset(vpl_f, 0.0).then_inc(zeroed, 1)
            rstd_of(1, 0)

            def heads(t, k):
                return t[:, k, 0:HKV].rearrange("p (h w) -> p h w", h=H)

            def subtract_max(j, b, u):
                k = 2 * b + u
                pool.wait_ge(s_max, 2 * num(j, b) + u + 1)
                pool.tensor_tensor(heads(sc, k), heads(sc, k),
                                   smax[:, k, :].unsqueeze(2).broadcast_to([P, H, KV]),
                                   ALU.subtract).then_inc(s_sub, 1)

            def normalise(j, b, u):
                k = 2 * b + u
                pool.wait_ge(s_rec, 2 * num(j, b) + u + 1)
                pool.tensor_tensor(heads(sc, k), heads(sc, k),
                                   rsum[:, k, :].unsqueeze(2).broadcast_to([P, H, KV]),
                                   ALU.mult).then_inc(s_norm, 1)

            def x_plus_bo(j, b, u):
                k = 2 * b + u
                pool.wait_ge(in_xb[k], 16 * (j + 1))
                pool.tensor_tensor(xb[:, k, :], xb[:, k, :], bias_row[:, :], ALU.add).then_inc(xb_done, 1)

            def rstd2_of(j, b):
                n = 2 * j + b
                pool.wait_ge(mv2, UB * (n + 1))
                until(pool, z2_done, UB * n)
                pool.tensor_tensor(var_b[:, :, 0], mv_b[:, :, 1], eps_c[:, :], ALU.add).then_inc(var2, 1)
                pool.wait_ge(var2, n + 1)
                pool.tensor_tensor(rstd_b[:, :, 0], var_b[:, :, 0], mhalf[:, :], ALU.pow).then_inc(rstd2, 1)

            pool.wait_ge(in_bo, 16)

            def body(j):
                for b in range(2):
                    if there(NA, j, b, -1):
                        normalise(*shift(j, b, -1), 1)
                    if there(NA, j, b, 0):
                        subtract_max(j, b, 0)
                    if there(NA, j, b, -1):
                        x_plus_bo(*shift(j, b, -1), 0)
                        x_plus_bo(*shift(j, b, -1), 1)
                    if is_block(NA - 1, j, b):
                        rstd2_of(0, 0)
                    if there(NA, j, b, 0):
                        subtract_max(j, b, 1)
                        normalise(j, b, 0)
                    if is_block(0, j, b):
                        pool.wait_ge(vb_hi, 1)
                        for bb in range(B):
                            last = pool.tensor_tensor(vblk[:, bb, 1, :, :], vpl_f[:, bb, :, :],
                                                      vblk[:, bb, 0, :, :].bitcast(F32), ALU.subtract)
                        last.then_inc(vb_lo, 1)
                    if there(NA, j, b, 3):
                        rstd_of(*shift(j, b, 3))

            pairs(pool, NA, body)

            def y_plus_b2(j, b, t):
                if t == 0:
                    pool.wait_ge(in_y[b], 16 * (j + 1))
                    until(pool, outs[b], 16 * UB * j)
                pool.tensor_tensor(yb[b][:, t, :], ya[b][:, t, :], bias_row[:, :], ALU.add).then_inc(yb_done, 1)

            pool.wait_ge(in_b2, 16)
            pool.wait_ge(ffn_lo[3], 1)
            for t in range(UB):
                y_plus_b2(0, 0, t)
            rstd2_of(0, 1)
            for k in range(4):
                pool.wait_ge(y_out[k], 16 * (NA // 2))

            def body2(j):
                for b in range(2):
                    for c in range(NFF):
                        if c % 2 and there(NB, j, b, 0):
                            pool.wait_ge(h_hi_act, 8 * num(j, b) + c // 2 + 1)
                            pool.tensor_tensor(hs[:, c % 4, 1, :], hg[:, c % 4, :],
                                               hs[:, c % 4, 0, :].bitcast(F32), ALU.subtract)\
                                .then_inc(h_lo_pool, 1)
                        if c == 11 and there(NB, j, b, 2):
                            rstd2_of(j + 1, b)
                        if c in (12, 13, 14, 15) and there(NB, j, b, 1):
                            y_plus_b2(*shift(j, b, 1), c - 12)

            pairs(pool, NB, body2)

        @block.scalar
        def _(act):
            act.dma_start(ctx_f, ctx.rearrange("b k c -> k b c")).then_inc(in_ctx, 16)
            for row, v in ((0, bq), (G, bk), (2 * G, b1)):
                n = v.shape[0] // P
                act.dma_start(bias_f[row:row + n, :], v.rearrange("(g p) -> g p", p=P)).then_inc(in_bias, 16)
            act.dma_start(bias_row[:, :], bv.partition_broadcast(P)).then_inc(in_bv, 16)

            def turned_z(j, b):
                n = 2 * j + b
                for u, bk_ in ((0, B6), (1, B4)):
                    act.wait_ge(zt_full, 2 * n + u + 1)
                    act.activation(zt[:, 0, :, u * P:(u + 1) * P],
                                   bk_[:, :].rearrange("p (k t) -> p k t", k=KD), ACT.Copy).then_inc(zt_hi, 1)

            def q_high(j, b, half):
                n = 2 * j + b
                act.wait_ge(q_full, 2 * n + half + 1)
                for i in range(2):
                    g = 2 * half + i
                    hi = act.activation(qt[:, b, 0, g, :], B4[:, i * TA:(i + 1) * TA], ACT.Identity,
                                        bias=bqs_c[:, g:g + 1])
                hi.then_inc(q_hi, 1)

            act.wait_ge(in_wq, 16)
            act.activation(wq_r[:, 0, :, :], wq_f, ACT.Copy, scale=SCALE).then_inc(wq_hi, 1)
            turned_z(0, 0)
            act.wait_ge(k_copied, 1)
            act.wait_ge(zeroed, 1)
            for dst, src in k_heads(0):
                last = act.activation(dst, src, ACT.Copy)
            last.then_inc(kb_hi, 1)
            act.wait_ge(bqs_ready, 1)
            q_high(0, 0, 0)
            q_high(0, 0, 1)
            act.wait_ge(v_copied, 2)
            act.dma_start(bias_row[:, :], bo.partition_broadcast(P)).then_inc(in_bo, 16)
            turned_z(0, 1)

            def probs_high(j, b, u, parts):
                s = 2 * (2 * j + b) + u
                for part in parts:
                    c0, bk_ = 4 * part, (B5, B6, B5)[part]
                    nch = min(4, NCH - c0)
                    act.wait_ge(pt_full, 3 * s + (part + 1))
                    act.activation(pt[:, 0, c0:c0 + nch, u * P:(u + 1) * P],
                                   bk_[:, 0:nch * P].rearrange("p (c t) -> p c t", c=nch),
                                   ACT.Copy).then_inc(pt_hi, 1)

            def exponent(j, b, u):
                k = 2 * b + u
                act.wait_ge(s_sub, 2 * num(j, b) + u + 1)
                act.activation(sc[:, k, 0:HKV], sc[:, k, 0:HKV], ACT.Exp).then_inc(s_exp, 1)

            def heads_high(j, b):
                n = 2 * j + b
                for half, bk_ in ((0, B5), (1, B6)):
                    act.wait_ge(pv_full, 2 * n + half + 1)
                    act.activation(ot[:, 0, 2 * half:2 * half + 2, :],
                                   bk_[:, :].rearrange("p (g t) -> p g t", g=2), ACT.Copy).then_inc(ot_hi, 1)

            def ffn_high(i):
                hi, src = ((u1_r[:, 0, :, :], u1_f), (v1_r[:, 0, :], v1_f), (v2_r[:, 0, :], v2_f),
                           (u2_r[:, 0, :, :], u2_f))[i]
                act.activation(hi, src, ACT.Copy).then_inc(ffn_hi[i], 1)

            def turned_z2(j, b, t):
                act.wait_ge(z2t_full, UB * (2 * j + b) + t + 1)
                act.activation(z2t[:, 0, :, t * P:(t + 1) * P],
                               z2_bank(j, b, t).rearrange("p (k t) -> p k t", k=KD),
                               ACT.Copy).then_inc(z2t_hi, 1)

            def p1_high(j, b):
                act.wait_ge(p1_full, 2 * j + b + 1)
                act.activation(p1t[:, b, 0, :], p1_bank(j, b)[:, :], ACT.Copy).then_inc(p1_hi, 1)

            def body(j):
                for b in range(2):
                    before, after = there(NA, j, b, -1), there(NA, j, b, 1)
                    for u in range(2):
                        if before:
                            probs_high(*shift(j, b, -1), u, (0, 1))
                        if after:
                            q_high(*shift(j, b, 1), u)
                        if before:
                            probs_high(*shift(j, b, -1), u, (2,))
                        if u == 0 and is_block(0, j, b):
                            act.wait_ge(in_wo, 16)
                            act.activation(wo_r[:, 0, :, :], wo_f, ACT.Copy).then_inc(wo_hi, 1)
                        if u == 0 and there(NA, j, b, 0):
                            exponent(j, b, 0)
                    if there(NA, j, b, 2):
                        turned_z(j + 1, b)
                    if is_block(NA - 2, j, b):
                        act.wait_ge(q_full, 2 * NA)
                        act.wait_ge(in_ffn, 4 * 16)
                        ffn_high(0)
                        ffn_high(2)
                    if is_block(NA - 1, j, b):
                        act.wait_ge(s_full, 2 * NA)
                        ffn_high(1)
                        for t in range(UB):
                            turned_z2(0, 0, t)
                    if there(NA, j, b, 0):
                        exponent(j, b, 1)
                    if is_block(0, j, b):
                        act.wait_ge(v_placed, 16 * N_PIECES)
                        for bb in range(B):
                            hi = act.activation(vblk[:, bb, 0, :, :], vpl_f[:, bb, :, :], ACT.Copy)
                        hi.then_inc(vb_hi, 1)
                    if before:
                        heads_high(*shift(j, b, -1))
                    if is_block(NA - 1, j, b):
                        p1_high(0, 0)
                    if is_block(NA, j, b):
                        ffn_high(3)

            pairs(act, NA, body)

            act.wait_ge(xb_done, 2 * NA)
            act.dma_start(bias_row[:, :], b2.partition_broadcast(P)).then_inc(in_b2, 16)

            def q2_high(j, b):
                act.wait_ge(u2_done, NFF * (2 * j + b + 1))
                act.activation(q2t[:, 0, :], (B4, B5)[b][:, :], ACT.Copy).then_inc(q2_hi, 1)

            def body2(j):
                for b in range(2):
                    for c in range(NFF):
                        if there(NB, j, b, 0):
                            n = NFF * num(j, b) + c
                            act.wait_ge(h_full, n + 1)
                            if not isinstance(j, int) or n >= 4:
                                if c % 2:
                                    act.wait_ge(h_lo_pool, 8 * num(j, b) + (c + 1) // 2 - 2)
                                else:
                                    act.wait_ge(h_lo, 8 * num(j, b) + c // 2 - 1)
                            act.activation(hg[:, c % 4, :], ps_s[:, c % 4, :], ACT.Gelu_apprx_tanh,
                                           bias=b1_c[:, c:c + 1]).then_inc(h_gelu, 1)
                            if c % 2:
                                if not isinstance(j, int) or n >= 4:
                                    act.wait_ge(u2_done, n - 3)
                                act.wait_ge(h_gelu, n + 1)
                                act.activation(hs[:, c % 4, 0, :], hg[:, c % 4, :], ACT.Copy)\
                                   .then_inc(h_hi_act, 1)
                        if c == 3 and there(NB, j, b, -1):
                            q2_high(*shift(j, b, -1))
                        if c in TURNS and there(NB, j, b, 1):
                            turned_z2(*shift(j, b, 1), TURNS.index(c))
                        if c == 13 and there(NB, j, b, 1):
                            p1_high(*shift(j, b, 1))

            pairs(act, NB, body2)

        @block.vector
        def _(dve):
            def norm_stats(j, b, u):
                k = 2 * b + u
                n = 2 * (2 * j + b) + u
                dve.wait_ge(in_x[k], 16 * (j + 1))
                until(dve, z_done, n - 3)
                dve.bn_stats(stats[:, k, :], xa[:, k, :]).then_inc(stats_done, 1)
                dve.wait_ge(stats_done, n + 1)
                dve.memset(stall[:, :], 0.0)
                dve.bn_aggr(mv[:, k, :], stats[:, k, :]).then_inc(mv_done, 1)

            def norm_z(j, b):
                n = 2 * j + b
                dve.wait_ge(rstd_done, n + 1)
                for u in range(2):
                    k = 2 * b + u
                    until(dve, zt_full, 2 * n + u - 1)
                    dve.tensor_scalar(z[:, u, :], xa[:, k, :], mv[:, k, 0:1], rstd[:, k:k + 1],
                                      ALU.subtract, ALU.mult).then_inc(z_done, 1)

            def turned_z(j, b):
                n = 2 * j + b
                for u, bk_ in ((0, B6), (1, B4)):
                    dve.wait_ge(zt_hi, 2 * n + u + 1)
                    dve.tensor_tensor(zt[:, 1, :, u * P:(u + 1) * P],
                                      bk_[:, :].rearrange("p (k t) -> p k t", k=KD),
                                      zt[:, 0, :, u * P:(u + 1) * P].bitcast(F32),
                                      ALU.subtract).then_inc(zt_lo, 1)

            def q_low(j, b, half):
                n = 2 * j + b
                dve.wait_ge(q_hi, 2 * n + half + 1)
                for i in range(2):
                    g = 2 * half + i
                    lo = dve.scalar_tensor_tensor(qt[:, b, 1, g, :], B4[:, i * TA:(i + 1) * TA],
                                                  bqs_c[:, g:g + 1], qt[:, b, 0, g, :].bitcast(F32),
                                                  ALU.add, ALU.subtract)
                lo.then_inc(q_lo, 1)

            norm_stats(0, 0, 0)
            norm_stats(0, 0, 1)
            norm_z(0, 0)
            dve.wait_ge(bias_turned, 1)
            dve.tensor_scalar(bqs_c[:, :], B5[:, 0:G], SCALE, None, ALU.mult)
            dve.tensor_copy(bk_c[:, :], B5[:, G:2 * G])
            dve.tensor_copy(b1_c[:, :], B5[:, 2 * G:2 * G + NFF]).then_inc(bqs_ready, 1)
            dve.wait_ge(ctx_turned, 1)
            dve.tensor_copy(once[:, 0:KC * B * KV], B7[:, 0:KC * B * KV]).then_inc(ctx_copied, 1)
            turned_z(0, 0)
            dve.wait_ge(wq_hi, 1)
            dve.scalar_tensor_tensor(wq_r[:, 1, :, :].rearrange("p k n -> p (k n)"),
                                     wq_f.rearrange("p k n -> p (k n)"), SCALE,
                                     wq_r[:, 0, :, :].rearrange("p k n -> p (k n)").bitcast(F32),
                                     ALU.mult, ALU.subtract).then_inc(wq_lo, 1)
            dve.wait_ge(k_full, 1)
            dve.wait_ge(bqs_ready, 1)
            for g in range(G):
                src = ps_s[:, g // 3, (g % 3) * B * KV:(g % 3 + 1) * B * KV]
                last = dve.tensor_scalar(kt_f[:, g, :, :].rearrange("p b w -> p (b w)"), src,
                                         bk_c[:, g:g + 1], None, ALU.add)
            last.then_inc(k_copied, 1)
            dve.wait_ge(kb_hi, 1)
            for (dst, src), (hi, _) in zip(k_heads(1), k_heads(0)):
                last = dve.tensor_tensor(dst, src, hi.bitcast(F32), ALU.subtract)
            last.then_inc(kb_lo, 1)
            norm_stats(0, 1, 0)
            norm_stats(0, 1, 1)
            norm_z(0, 1)
            dve.wait_ge(bqs_ready, 1)
            q_low(0, 0, 0)
            q_low(0, 0, 1)
            dve.wait_ge(in_bv, 16)
            for b in range(B):
                dve.wait_ge(v_full, b + 1)
                dve.tensor_tensor(v_f[:, b, :], ps_s[0:KV, 2 + b, :], bias_row[0:KV, :],
                                  ALU.add).then_inc(v_copied, 1)
            for k in range(4):
                last = dve.memset(sc[:, k, HKV:], 0.0)
            last.then_inc(pad_zero, 1)
            turned_z(0, 1)
            norm_stats(1, 0, 0)
            norm_stats(1, 0, 1)

            def clip(j, b, u):
                k, s = 2 * b + u, 2 * (2 * j + b) + u
                dve.wait_ge(s_full, s + 1)
                until(dve, pt_full, 3 * (s - 3))
                dve.tensor_scalar(sc[:, k, 0:HKV].rearrange("p (g w) -> p g w", g=G), ps_s[:, :, 0:GW],
                                  CLAMP, -CLAMP, ALU.min, ALU.max).then_inc(s_clip, 1)

            def heads(k):
                return sc[:, k, 0:HKV].rearrange("p (h w) -> p h w", h=H)

            def maxima(j, b, u):
                k, s = 2 * b + u, 2 * (2 * j + b) + u
                dve.wait_ge(s_clip, s + 1)
                dve.tensor_reduce(smax[:, k, :], heads(k), AX.X, ALU.max).then_inc(s_max, 1)

            def sums(j, b, u):
                k, s = 2 * b + u, 2 * (2 * j + b) + u
                dve.wait_ge(s_exp, s + 1)
                dve.tensor_reduce(ssum[:, k, :], heads(k), AX.X, ALU.add).then_inc(s_sum, 1)
                dve.wait_ge(s_sum, s + 1)
                dve.reciprocal(rsum[:, k, :], ssum[:, k, :]).then_inc(s_rec, 1)

            def probs_low(j, b, u, parts):
                s = 2 * (2 * j + b) + u
                for part in parts:
                    c0, bk_ = 4 * part, (B5, B6, B5)[part]
                    nch = min(4, NCH - c0)
                    dve.wait_ge(pt_hi, 3 * s + (part + 1))
                    dve.tensor_tensor(pt[:, 1, c0:c0 + nch, u * P:(u + 1) * P],
                                      bk_[:, 0:nch * P].rearrange("p (c t) -> p c t", c=nch),
                                      pt[:, 0, c0:c0 + nch, u * P:(u + 1) * P].bitcast(F32),
                                      ALU.subtract).then_inc(pt_lo, 1)

            def heads_low(j, b):
                n = 2 * j + b
                for half, bk_ in ((0, B5), (1, B6)):
                    dve.wait_ge(ot_hi, 2 * n + half + 1)
                    dve.tensor_tensor(ot[:, 1, 2 * half:2 * half + 2, :],
                                      bk_[:, :].rearrange("p (g t) -> p g t", g=2),
                                      ot[:, 0, 2 * half:2 * half + 2, :].bitcast(F32),
                                      ALU.subtract).then_inc(ot_lo, 1)

            def y_sum(j, b, u):
                k, s = 2 * b + u, 2 * (2 * j + b) + u
                dve.wait_ge(o_full, s + 1)
                dve.wait_ge(xb_done, s + 1)
                dve.tensor_tensor(xb[:, k, :], B7[:, :], xb[:, k, :], ALU.add).then_inc(y_done, 1)

            def ffn_low(i):
                lo, src, hi = ((u1_r[:, 1, :, :], u1_f, u1_r[:, 0, :, :]), (v1_r[:, 1, :], v1_f, v1_r[:, 0, :]),
                               (v2_r[:, 1, :], v2_f, v2_r[:, 0, :]), (u2_r[:, 1, :, :], u2_f, u2_r[:, 0, :, :]))[i]
                dve.wait_ge(ffn_hi[i], 1)
                dve.tensor_tensor(lo, src, hi.bitcast(F32), ALU.subtract).then_inc(ffn_lo[i], 1)

            def norm_stats2(j, b, t):
                n = UB * (2 * j + b) + t
                dve.wait_ge(in_y[b], 16 * (j + 1))
                dve.bn_stats(stats_b[:, t, :], ya[b][:, t, :]).then_inc(stats2, 1)
                dve.wait_ge(stats2, n + 1)
                dve.memset(stall[:, :], 0.0)
                dve.bn_aggr(mv_b[:, t, :], stats_b[:, t, :]).then_inc(mv2, 1)

            def norm_z2(j, b, t):
                n = 2 * j + b
                dve.wait_ge(rstd2, n + 1)
                until(dve, z2t_full, UB * (n - 1) + t + 1)
                dve.tensor_scalar(z2[:, t, :], ya[b][:, t, :], mv_b[:, t, 0:1], rstd_b[:, t, :],
                                  ALU.subtract, ALU.mult).then_inc(z2_done, 1)

            def turned_z2(j, b, t):
                dve.wait_ge(z2t_hi, UB * (2 * j + b) + t + 1)
                dve.tensor_tensor(z2t[:, 1, :, t * P:(t + 1) * P],
                                  z2_bank(j, b, t).rearrange("p (k t) -> p k t", k=KD),
                                  z2t[:, 0, :, t * P:(t + 1) * P].bitcast(F32),
                                  ALU.subtract).then_inc(z2t_lo, 1)

            def p1_low(j, b):
                dve.wait_ge(p1_hi, 2 * j + b + 1)
                dve.tensor_tensor(p1t[:, b, 1, :], p1_bank(j, b)[:, :], p1t[:, b, 0, :].bitcast(F32),
                                  ALU.subtract).then_inc(p1_lo, 1)

            def body(j):
                for b in range(2):
                    here, before, after = there(NA, j, b, 0), there(NA, j, b, -1), there(NA, j, b, 1)
                    for u in range(2):
                        if here:
                            clip(j, b, u)
                        if before:
                            probs_low(*shift(j, b, -1), u, (0,))
                        if here:
                            maxima(j, b, u)
                        if before:
                            probs_low(*shift(j, b, -1), u, (1,))
                        if u == 1 and here:
                            sums(j, b, 0)
                        if after:
                            q_low(*shift(j, b, 1), u)
                        if before:
                            probs_low(*shift(j, b, -1), u, (2,))
                        if u == 0 and is_block(0, j, b):
                            dve.wait_ge(wo_hi, 1)
                            dve.tensor_tensor(wo_r[:, 1, :, :], wo_f, wo_r[:, 0, :, :].bitcast(F32),
                                              ALU.subtract).then_inc(wo_lo, 1)
                        if u == 0 and there(NA, j, b, 2):
                            norm_z(j + 1, b)
                        if there(NA, j, b, -2):
                            y_sum(j - 1, b, u)
                        if there(NA, j, b, 3):
                            norm_stats(*shift(j, b, 3), u)
                        if u == 0 and is_block(NA - 1, j, b):
                            for t in range(UB):
                                norm_z2(0, 0, t)
                    if there(NA, j, b, 2):
                        turned_z(j + 1, b)
                    if is_block(NA - 2, j, b):
                        for t in range(UB):
                            norm_stats2(0, 0, t)
                        ffn_low(0)
                        ffn_low(2)
                    if is_block(NA - 1, j, b):
                        for t in range(UB):
                            turned_z2(0, 0, t)
                    if here:
                        sums(j, b, 1)
                    if is_block(NA - 1, j, b):
                        ffn_low(1)
                    if before:
                        heads_low(*shift(j, b, -1))
                    if is_block(NA - 1, j, b):
                        p1_low(0, 0)
                    if is_block(NA, j, b):
                        ffn_low(3)

            pairs(dve, NA, body)

            def q2_low(j, b):
                dve.wait_ge(q2_hi, 2 * j + b + 1)
                dve.tensor_tensor(q2t[:, 1, :], (B4, B5)[b][:, :], q2t[:, 0, :].bitcast(F32),
                                  ALU.subtract).then_inc(q2_lo, 1)

            def out_sum(j, b, t):
                n = UB * (2 * j + b) + t
                dve.wait_ge(o2_full, n + 1)
                dve.wait_ge(yb_done, n + 1)
                dve.tensor_tensor(yb[b][:, t, :], B7[:, :], yb[b][:, t, :],
                                  ALU.add).then_inc(o2_done, 1)

            for t in range(UB):
                norm_stats2(0, 1, t)
            for t in range(UB):
                norm_z2(0, 1, t)

            def body2(j):
                for b in range(2):
                    for c in range(NFF):
                        if there(NB, j, b, 0):
                            n = NFF * num(j, b) + c
                            if c % 2 == 0:
                                dve.wait_ge(h_gelu, n + 1)
                                if not isinstance(j, int) or n >= 4:
                                    dve.wait_ge(u2_done, n - 3)
                                dve.tensor_copy(hs[:, c % 4, 0, :], hg[:, c % 4, :]).then_inc(h_hi, 1)
                                dve.wait_ge(h_hi, 8 * num(j, b) + c // 2 + 1)
                                dve.tensor_tensor(hs[:, c % 4, 1, :], hg[:, c % 4, :],
                                                  hs[:, c % 4, 0, :].bitcast(F32), ALU.subtract)\
                                    .then_inc(h_lo, 1)
                        if c == 3 and there(NB, j, b, -1):
                            q2_low(*shift(j, b, -1))
                        if c in TURNS and there(NB, j, b, 1):
                            turned_z2(*shift(j, b, 1), TURNS.index(c))
                        if c in DOWNS and there(NB, j, b, -1):
                            out_sum(*shift(j, b, -1), DOWNS.index(c))
                        if c in (7, 8, 9, 10) and there(NB, j, b, 2):
                            norm_stats2(j + 1, b, c - 7)
                        if c in (12, 13, 14, 15) and there(NB, j, b, 2):
                            norm_z2(j + 1, b, c - 12)
                        if c == 13 and there(NB, j, b, 1):
                            p1_low(*shift(j, b, 1))

            pairs(dve, NB, body2)

        @block.tensor
        def _(pe):
            def product(ps, lhs, rhs, first=True, last=True):
                for i, (a, c) in enumerate(PASSES):
                    mm = pe.matmul(ps, lhs(a), rhs(c), start=first and i == 0,
                                   stop=last and i == len(PASSES) - 1)
                return mm

            def turn_z(j, b):
                n = 2 * j + b
                for u, bk_ in ((0, B6), (1, B4)):
                    pe.wait_ge(z_done, 2 * n + u + 1)
                    if u == 0:
                        if isinstance(j, int) and n < 3:
                            until(pe, zt_lo, 2 * n - 1)
                        else:
                            pe.wait_ge(pt_lo, 6 * n - 13)
                    else:
                        until(pe, q_lo, 2 * n)
                    for k in range(KD):
                        last = pe.transpose(bk_[:, k * P:(k + 1) * P], z[:, u, k * P:(k + 1) * P],
                                            ident[:, :])
                    last.then_inc(zt_full, 1)

            def project_q(j, b, half):
                n = 2 * j + b
                pe.wait_ge(zt_lo, 2 * n + 2)
                if half:
                    pe.wait_ge(q_lo, 2 * n + 1)
                for i in range(2):
                    g = 2 * half + i
                    for k in range(KD):
                        last = product(B4[:, i * TA:(i + 1) * TA],
                                       lambda a: wq_r[:, a, k, g * P:(g + 1) * P],
                                       lambda a: zt[:, a, k, :], k == 0, k == KD - 1)
                last.then_inc(q_full, 1)

            def scores(j, b, u):
                n = 2 * j + b
                pe.wait_ge(q_lo, 2 * n + 2)
                until(pe, s_clip, 2 * n + u)
                for g in range(G):
                    last = product(ps_s[:, g, 0:GW], lambda a: qt[:, b, a, g, u * P:(u + 1) * P],
                                   lambda a: kblk[:, b, a, g, :])
                last.then_inc(s_full, 1)

            def turn_probs(j, b, u, parts):
                k, n = 2 * b + u, 2 * j + b
                s = 2 * n + u
                for part in parts:
                    bk_ = (B5, B6, B5)[part]
                    if part == 0:
                        pe.wait_ge(s_norm, s + 1)
                        if u == 0:
                            until(pe, ot_lo, 2 * n - 1)
                        else:
                            pe.wait_ge(pt_lo, 3 * s)
                    elif part == 1 and u == 0:
                        if isinstance(j, int) and n == 0:
                            pe.wait_ge(zt_lo, 5)
                        else:
                            pe.wait_ge(ot_lo, 2 * n)
                    elif part == 2:
                        pe.wait_ge(pt_lo, 3 * s + 1)
                    for c in range(4 * part, min(4 * part + 4, NCH)):
                        last = pe.transpose(bk_[:, (c % 4) * P:(c % 4 + 1) * P],
                                            sc[:, k, c * P:(c + 1) * P], ident[:, :])
                    last.then_inc(pt_full, 1)

            def weigh_values(j, b):
                n = 2 * j + b
                pe.wait_ge(pt_lo, 6 * n + 6)
                for half, bk_ in ((0, B5), (1, B6)):
                    if half and (not isinstance(j, int) or n + 3 < NA):
                        pe.wait_ge(zt_lo, 2 * (n + 3) + 1)
                    for i in range(2):
                        g = 2 * half + i
                        mine = [(q, c) for q, (c, gg) in enumerate(PAIRS) if gg == g]
                        for q, c in mine:
                            last = product(bk_[:, i * TA:(i + 1) * TA], lambda a: vblk[:, b, a, q, :],
                                           lambda a: pt[:, a, c, :], q == mine[0][0], q == mine[-1][0])
                    last.then_inc(pv_full, 1)

            def project_out(j, b, u):
                n = 2 * j + b
                pe.wait_ge(ot_lo, 2 * n + 2)
                until(pe, y_done, 2 * n + u)
                for k in range(KD):
                    last = product(B7[:, :], lambda a: ot[:, a, k, u * P:(u + 1) * P],
                                   lambda a: wo_r[:, a, k, :], k == 0, k == KD - 1)
                last.then_inc(o_full, 1)

            def turn_z2(j, b, t):
                n = 2 * j + b
                pe.wait_ge(z2_done, UB * n + t + 1)
                if is_block(0, j, b):
                    until(pe, z2t_lo, t - 1)
                elif t == 0:
                    until(pe, p1_lo, n)
                else:
                    pe.wait_ge(z2t_lo, UB * n + t)
                for k in range(KD):
                    last = pe.transpose(z2_bank(j, b, t)[:, k * P:(k + 1) * P], z2[:, t, k * P:(k + 1) * P],
                                        ident[:, :])
                last.then_inc(z2t_full, 1)

            def project_u1(j, b):
                n = 2 * j + b
                pe.wait_ge(z2t_lo, UB * (n + 1))
                for k in range(KD):
                    last = product(p1_bank(j, b)[:, :], lambda a: u1_r[:, a, k, :], lambda a: z2t[:, a, k, :],
                                   k == 0, k == KD - 1)
                last.then_inc(p1_full, 1)

            pe.wait_ge(const_ready, 4)
            pe.wait_ge(in_bias, 3 * 16)
            pe.transpose(B5[:, 0:2 * G + NFF], bias_f[:, :], ident[0:2 * G + NFF, 0:2 * G + NFF])\
              .then_inc(bias_turned, 1)
            pe.wait_ge(in_ctx, 16)
            for k in range(KC):
                for b in range(B):
                    o = (k * B + b) * KV
                    last = pe.transpose(B7[:, o:o + KV], ctx_f[:, b, k * P:(k + 1) * P], ident[0:KV, 0:KV])
            last.then_inc(ctx_turned, 1)
            turn_z(0, 0)
            pe.wait_ge(ctx_copied, 1)
            pe.wait_ge(in_wk, 16)
            for g in range(G):
                for k in range(KC):
                    last = pe.matmul(ps_s[:, g // 3, (g % 3) * B * KV:(g % 3 + 1) * B * KV],
                                     wk_f[:, k, g * P:(g + 1) * P],
                                     ctxt_f[:, k, :, :].rearrange("p b w -> p (b w)"),
                                     start=k == 0, stop=k == KC - 1)
            last.then_inc(k_full, 1)
            pe.wait_ge(wq_lo, 1)
            project_q(0, 0, 0)
            project_q(0, 0, 1)
            pe.wait_ge(in_wv, 16)
            for b in range(B):
                for k in range(KC):
                    last = pe.matmul(ps_s[0:KV, 2 + b, :], ctxt_f[:, k, b, :], wv_f[:, k, :],
                                     start=k == 0, stop=k == KC - 1)
                last.then_inc(v_full, 1)
            turn_z(0, 1)
            pe.wait_ge(kb_lo, 1)
            pe.wait_ge(v_copied, 2)

            def body(j):
                for b in range(2):
                    here, before, after = there(NA, j, b, 0), there(NA, j, b, -1), there(NA, j, b, 1)
                    for u in range(2):
                        if here:
                            scores(j, b, u)
                        if before:
                            if isinstance(j, int) and num(j, b, -1) == 0 and u == 0:
                                pe.wait_ge(pad_zero, 1)
                            turn_probs(*shift(j, b, -1), u, (0, 1))
                        if after:
                            project_q(*shift(j, b, 1), u)
                        if before:
                            turn_probs(*shift(j, b, -1), u, (2,))
                        if there(NA, j, b, -2):
                            if isinstance(j, int) and num(j, b, -2) == 0 and u == 0:
                                pe.wait_ge(wo_lo, 1)
                            project_out(j - 1, b, u)
                    if there(NA, j, b, 2):
                        turn_z(j + 1, b)
                    if is_block(NA - 1, j, b):
                        pe.wait_ge(s_clip, 2 * NA)
                        for t in range(UB):
                            turn_z2(0, 0, t)
                    if before:
                        if isinstance(j, int) and num(j, b, -1) == 0:
                            pe.wait_ge(vb_lo, 1)
                        weigh_values(*shift(j, b, -1))
                    if is_block(NA - 1, j, b):
                        pe.wait_ge(ffn_lo[0], 1)
                        project_u1(0, 0)

            pairs(pe, NA, body)

            def hidden(j, b, c):
                n = 2 * j + b
                if c == 0:
                    pe.wait_ge(p1_lo, n + 1)
                if not isinstance(j, int) or NFF * n + c >= 4:
                    pe.wait_ge(h_gelu, NFF * n + c - 3)
                product(ps_s[:, c % 4, :], lambda a: v1_r[:, a, c * P:(c + 1) * P],
                        lambda a: p1t[:, b, a, :]).then_inc(h_full, 1)

            def project_u2(j, b, c):
                n = 2 * j + b
                if c % 2:
                    pe.wait_ge(h_lo_pool, 8 * n + (c + 1) // 2)
                else:
                    pe.wait_ge(h_lo, 8 * n + c // 2 + 1)
                if c == 0:
                    until(pe, q2_lo, n - 1)
                product((B4, B5)[b][:, :], lambda a: u2_r[:, a, c, :], lambda a: hs[:, c % 4, a, :],
                        c == 0, c == NFF - 1).then_inc(u2_done, 1)

            def project_v2(j, b, t):
                n = 2 * j + b
                pe.wait_ge(q2_lo, n + 1)
                until(pe, o2_done, UB * n + t)
                product(B7[:, :], lambda a: q2t[:, a, t * P:(t + 1) * P],
                        lambda a: v2_r[:, a, :]).then_inc(o2_full, 1)

            for i in range(1, 4):
                pe.wait_ge(ffn_lo[i], 1)
            pe.wait_ge(y_done, 2 * NA)

            def body2(j):
                for b in range(2):
                    for c in range(NFF):
                        if there(NB, j, b, 0):
                            hidden(j, b, c)
                        if c >= 3 and there(NB, j, b, 0):
                            project_u2(j, b, c - 3)
                        if c < 3 and there(NB, j, b, -1):
                            project_u2(*shift(j, b, -1), NFF + c - 3)
                        if c in TURNS and there(NB, j, b, 1):
                            turn_z2(*shift(j, b, 1), TURNS.index(c))
                        if c in DOWNS and there(NB, j, b, -1):
                            project_v2(*shift(j, b, -1), DOWNS.index(c))
                        if c == 12 and there(NB, j, b, 1):
                            project_u1(*shift(j, b, 1))

            pairs(pe, NB, body2)


_NAMES = ["x", "ctx_768", "L0_xattn_Wq", "L0_xattn_bq", "L0_xattn_Wk", "L0_xattn_bk", "L0_xattn_Wv",
          "L0_xattn_bv", "L0_xattn_Wo", "L0_xattn_bo", "L0_ffn_U1", "L0_ffn_V1", "L0_ffn_b1",
          "L0_ffn_U2", "L0_ffn_V2", "L0_ffn_b2"]


def kernel(**inputs):
    import numpy as np
    import concourse.bacc as bacc
    from concourse.bass_utils import run_bass_kernel_spmd

    nc = bacc.Bacc("TRN2", target_bir_lowering=False, num_devices=1)
    arrays, args = {}, []
    for name in _NAMES:
        a = np.ascontiguousarray(inputs[name])
        arrays[f"in_{name}"] = a
        args.append(nc.dram_tensor(f"in_{name}", a.shape, mybir.dt.from_np(a.dtype), kind="ExternalInput").ap())
    out = nc.dram_tensor("out", inputs["x"].shape, F32, kind="ExternalOutput").ap()
    xattn_ffn(nc, *args, out)
    r = run_bass_kernel_spmd(nc, [arrays], core_ids=[0])
    return r.results[0]["out"]
```

```python
import concourse.bass as bass
from concourse import mybir
from contextlib import ExitStack

F32 = mybir.dt.float32
F32R = mybir.dt.float32r
ALU = mybir.AluOpType
ACT = mybir.ActivationFunctionType
AX = mybir.AxisListType

P = 128
B, S, D = 2, 2048, 512
KV, CKV = 77, 384
H = 16
DH = D // H
GH = P // DH
G = H // GH
GW = GH * KV
HKV = H * KV
NCH = -(-HKV // P)
KD = D // P
KC = CKV // P
R, FF = 128, 2048
NFF = FF // P
EPS = 1e-5
CLAMP = 10000.0
SCALE = DH ** -0.5
PIECES = [(h, c) for h in range(H) for c in range(NCH) if c * P < (h + 1) * KV and (c + 1) * P > h * KV]
NP = len(PIECES)

TA = 256
NA = B * S // TA
TPB = S // P
TB = 512
UB = TB // P
NB = B * S // TB


def num(j, b, d=0):
    return 2 * j + (b + d)


def there(total, j, b, d):
    return not isinstance(j, int) or 0 <= 2 * j + b + d < total


def shift(j, b, d):
    return j + (b + d) // 2, (b + d) % 2


def is_block(n, j, b):
    return isinstance(j, int) and 2 * j + b == n


def until(eng, sem, value):
    if not isinstance(value, int) or value > 0:
        eng.wait_ge(sem, value)


def pairs(eng, total, body):
    head, tail = (2, 2) if total > 8 else (1, 1)
    for j in range(head):
        body(j)
    with eng.Fori(head, total // 2 - tail) as j:
        body(j)
    for j in range(total // 2 - tail, total // 2 + 1):
        body(j)


def xattn_ffn(nc, x, ctx, wq, bq, wk, bk, wv, bv, wo, bo, u1, v1, b1, u2, v2, b2, out):
    x_t = x.rearrange("b (t p) d -> (b t) p d", p=P)
    y_dram = nc.dram_tensor("y_between", [B * S, D], F32).ap()
    y_t = y_dram.rearrange("(t p) d -> t p d", p=P)
    y_b = y_dram.rearrange("(n t p) d -> n p t d", p=P, t=UB)
    out_t = out.rearrange("b (t p) d -> (b t) p d", p=P)

    stack = ExitStack()
    with stack:
        def sb(name, shape, dt=F32):
            return stack.enter_context(nc.sbuf_tensor(name, shape, dt))

        def sem(name):
            return stack.enter_context(nc.semaphore(name))

        wqo_r = sb("wqo_r", [P, 2 * 2 * KD * D], F32R)
        wq_r = wqo_r[:, 0:2 * KD * D].rearrange("p (h k n) -> p h k n", h=2, k=KD)
        wo_r = wqo_r[:, 2 * KD * D:].rearrange("p (h k n) -> p h k n", h=2, k=KD)
        kb_t = sb("kblk_r", [P, B * 2 * G * GW], F32R)
        kblk = kb_t[:, :].rearrange("p (b h g w) -> p b h g w", b=B, h=2, g=G)
        zt_t = sb("zt_r", [P, 2 * KD * TA], F32R)
        zt = zt_t[:, :].rearrange("p (h k t) -> p h k t", h=2, k=KD)
        qt_t = sb("qt_r", [P, 2 * 2 * G * TA], F32R)
        qt = qt_t[:, :].rearrange("p (b h g t) -> p b h g t", b=2, h=2, g=G)
        ot = sb("ot_r", [P, 2, G, TA], F32R)
        u2_r = sb("u2_r", [P, 2, NFF, R], F32R)
        hs = sb("hs_r", [P, 4, 2, TB], F32R)
        z2t = wqo_r[:, 0:2 * KD * TB].rearrange("p (h k t) -> p h k t", h=2, k=KD)
        u1_r = zt_t[:, 0:2 * KD * R].rearrange("p (h k n) -> p h k n", h=2, k=KD)
        v2_r = zt_t[:, 2 * KD * R:2 * KD * R + 2 * D].rearrange("p (h n) -> p h n", h=2)
        v1_r = kb_t[:, 0:2 * FF].rearrange("p (h n) -> p h n", h=2)
        p1t = qt_t[:, 0:4 * TB].rearrange("p (b h t) -> p b h t", b=2, h=2)
        q2t = qt_t[:, 4 * TB:6 * TB].rearrange("p (h t) -> p h t", h=2)

        xs = sb("xs", [P, 8 * D])
        xa = xs[:, 0:4 * D].rearrange("p (s d) -> p s d", s=4)
        xb = xs[:, 4 * D:].rearrange("p (s d) -> p s d", s=4)
        ss = sb("ss", [P, 4 * NCH * P])
        sc = ss[:, :].rearrange("p (s w) -> p s w", s=4)
        hg = ss[:, 0:4 * TB].rearrange("p (s t) -> p s t", s=4)
        fw = sb("fw", [P, 2 * FF + KD * R + D])
        z = sb("z", [P, 2, D])
        pt = sb("pt", [P, NCH, TA])
        vrows = sb("vrows", [P, B, NP, DH])
        wq_f = ss[:, 0:KD * D].rearrange("p (k n) -> p k n", k=KD)
        wv_f = ss[:, KD * D:KD * D + KC * D].rearrange("p (k n) -> p k n", k=KC)
        ctx_f = ss[0:KV, (KD + KC) * D:(KD + KC) * D + B * CKV].rearrange("p (b c) -> p b c", b=B)
        wo_f = xb
        wk_f = fw[:, 0:KC * D].rearrange("p (k n) -> p k n", k=KC)
        once = sb("once", [P, KC * B * KV + G * B * KV + B * D])
        ctxt_f = once[:, 0:KC * B * KV].rearrange("p (k b w) -> p k b w", k=KC, b=B)
        kt_f = once[:, KC * B * KV:(KC + G) * B * KV].rearrange("p (g b w) -> p g b w", g=G, b=B)
        v_f = once[0:KV, (KC + G) * B * KV:].rearrange("p (b d) -> p b d", b=B)
        z2 = once[:, 0:UB * D].rearrange("p (t d) -> p t d", t=UB)
        v1_f = fw[:, 0:FF]
        u2_f = fw[:, FF:2 * FF].rearrange("p (k n) -> p k n", k=NFF)
        u1_f = fw[:, 2 * FF:2 * FF + KD * R].rearrange("p (k n) -> p k n", k=KD)
        v2_f = fw[:, 2 * FF + KD * R:]
        ya = [xa, fw[:, 0:UB * D].rearrange("p (t d) -> p t d", t=UB)]
        yb = [fw[:, FF:FF + UB * D].rearrange("p (t d) -> p t d", t=UB), xb]
        bias_row = sb("bias_row", [P, D])
        bias_f = sb("bias_f", [2 * G + NFF, P])
        bias_c = sb("bias_c", [P, 2 * G + NFF])
        bq_c, bk_c, b1_c = bias_c[:, 0:G], bias_c[:, G:2 * G], bias_c[:, 2 * G:]
        ident = sb("ident", [P, P])
        mhalf = sb("mhalf", [P, UB])
        eps_c = sb("eps_c", [P, UB])
        stall = sb("stall", [P, 1])
        stats = sb("stats", [P, 4, 6])
        stats_b, mv_b, var_b, rstd_b = (sb(n, [P, UB, w]) for n, w in (
            ("stats_b", 6), ("mv_b", 2), ("var_b", 1), ("rstd_b", 1)))
        mv = sb("mv", [P, 4, 2])
        var_e = sb("var_e", [P, 4])
        rstd = sb("rstd", [P, 4])
        smax = sb("smax", [P, 4, H])
        ssum = sb("ssum", [P, 4, H])
        rsum = sb("rsum", [P, 4, H])

        bank = [stack.enter_context(nc.psum_tensor(f"bank{i}", [P, 512], F32)) for i in range(4, 8)]
        ps_s = stack.enter_context(nc.psum_tensor("ps_s", [P, 4, 512], F32))
        B4, B5, B6, B7 = bank
        z2_bank = lambda j, b, t: (B4[:, :], ps_s[:, 0, :])[t % 2] if is_block(0, j, b) else B6[:, :]
        p1_bank = lambda j, b: B4 if is_block(0, j, b) else B6

        in_x = [sem(f"in_x{i}") for i in range(4)]
        in_xb = [sem(f"in_xb{i}") for i in range(4)]
        y_out = [sem(f"y_out{i}") for i in range(4)]
        in_wk, in_wv, in_wo, in_ctx = (sem(n) for n in ("in_wk", "in_wv", "in_wo", "in_ctx"))
        in_wq = [sem(f"in_wq{i}") for i in range(2)]
        in_bias, in_bv, in_bo, in_b2, bias_turned = (sem(n) for n in ("in_bias", "in_bv", "in_bo", "in_b2", "bias_turned"))
        in_ffn, v_placed = sem("in_ffn"), sem("v_placed")
        const_ready, zeroed = sem("const_ready"), sem("zeroed")
        ctx_turned, ctx_copied, k_full, v_full, k_copied, v_copied = (
            sem(n) for n in ("ctx_turned", "ctx_copied", "k_full", "v_full", "k_copied", "v_copied"))
        wq_hi, wq_lo, wq_lo_pool, wo_hi, wo_lo, kb_hi, kb_lo, pad_zero, bias_ready = (
            sem(n) for n in ("wq_hi", "wq_lo", "wq_lo_pool", "wo_hi", "wo_lo", "kb_hi", "kb_lo",
                             "pad_zero", "bias_ready"))
        stats_done, mv_done, var_done, rstd_done, z_done = (
            sem(n) for n in ("stats_done", "mv_done", "var_done", "rstd_done", "z_done"))
        zt_full, zt_hi, zt_lo, q_full, q_hi, q_lo = (
            sem(n) for n in ("zt_full", "zt_hi", "zt_lo", "q_full", "q_hi", "q_lo"))
        s_full, s_clip, s_max, s_sub, s_exp, s_sum, s_rec, s_norm = (
            sem(n) for n in ("s_full", "s_clip", "s_max", "s_sub", "s_exp", "s_sum", "s_rec", "s_norm"))
        pt_full, pt_copied, pv_full, ot_hi, ot_lo, o_full, xb_done, y_done = (
            sem(n) for n in ("pt_full", "pt_copied", "pv_full", "ot_hi", "ot_lo", "o_full",
                             "xb_done", "y_done"))
        ffn_hi = [sem(f"ffn_hi_{n}") for n in ("u1", "v1", "v2", "u2")]
        ffn_lo = [sem(f"ffn_lo_{n}") for n in ("u1", "v1", "v2", "u2")]
        in_y = [sem(f"in_y{i}") for i in range(2)]
        outs = [sem(f"outs{i}") for i in range(2)]
        stats2, mv2, var2, rstd2, z2_done, yb_done = (
            sem(n) for n in ("stats2", "mv2", "var2", "rstd2", "z2_done", "yb_done"))
        z2t_full, z2t_hi, z2t_lo, p1_full, p1_hi, p1_lo = (
            sem(n) for n in ("z2t_full", "z2t_hi", "z2t_lo", "p1_full", "p1_hi", "p1_lo"))
        h_full, h_gelu, h_hi, h_hi_act, h_lo, h_lo_pool, u2_done, q2_hi, q2_lo, o2_full, o2_done = (
            sem(n) for n in ("h_full", "h_gelu", "h_hi", "h_hi_act", "h_lo", "h_lo_pool", "u2_done", "q2_hi", "q2_lo",
                             "o2_full", "o2_done"))

        PASSES = ((0, 0), (0, 1), (1, 0))

        def tile_row(j, b, u):
            return 2 * j + (b * TPB + u)

        def piece_rows(h, c):
            first, end = max(h * KV, c * P), min((h + 1) * KV, (c + 1) * P)
            return first - c * P, first - h * KV, end - first

        block = stack.enter_context(nc.Block())

        def k_heads(b, part):
            for i in range(GH):
                p0 = i * DH
                yield (kblk[p0:p0 + DH, b, part, :, i * KV:(i + 1) * KV], kt_f[p0:p0 + DH, :, b, :])

        wq_half = lambda w, half: w[:, :, half * D // 2:(half + 1) * D // 2]

        TURNS, DOWNS = (4, 6, 8, 10), (5, 7, 9, 11)
        EARLY = 4

        def early(j, b, c):
            return is_block(0, j, b) and c < EARLY

        @block.sync
        def _(sp):
            def held(value):
                return value if isinstance(value, int) else sp.snap(value)

            def load_x(j, b):
                jj, bb = j, b
                for u in range(2):
                    k = 2 * bb + u
                    row = held(tile_row(jj, bb, u))
                    until(sp, z_done, 2 * (2 * jj + bb - 2) + u + 1)
                    sp.dma_start(xa[:, k, :], x_t[row, :, :]).then_inc(in_x[k], 16)

            sp.dma_start(ctx_f, ctx.rearrange("b k c -> k b c")).then_inc(in_ctx, 16)
            load_x(0, 0)
            sp.dma_start(wk_f, wk.rearrange("(k p) n -> p k n", p=P)).then_inc(in_wk, 16)
            for half in range(2):
                sp.dma_start(wq_half(wq_f, half),
                             wq_half(wq.rearrange("(k p) n -> p k n", p=P), half)).then_inc(in_wq[half], 16)
            load_x(0, 1)
            sp.dma_start(wv_f, wv.rearrange("(k p) n -> p k n", p=P)).then_inc(in_wv, 16)
            sp.dma_start(wo_f, wo.rearrange("(k p) n -> p k n", p=P)).then_inc(in_wo, 16)
            load_x(1, 0)
            load_x(1, 1)
            sp.wait_ge(v_copied, 2)
            sp.wait_ge(zeroed, 2)
            for q, (h, c) in enumerate(PIECES):
                p0, kv0, n = piece_rows(h, c)
                sp.dma_start(vrows[p0:p0 + n, :, q, :],
                             v_f[kv0:kv0 + n, :, h * DH:(h + 1) * DH]).then_inc(v_placed, 16)

            def load_ffn():
                sp.wait_ge(k_full, 1)
                sp.dma_start(v1_f, v1).then_inc(in_ffn, 16)
                sp.dma_start(u2_f, u2.rearrange("(k p) n -> p k n", p=P)).then_inc(in_ffn, 16)
                sp.dma_start(u1_f, u1.rearrange("(k p) n -> p k n", p=P)).then_inc(in_ffn, 16)
                sp.dma_start(v2_f, v2).then_inc(in_ffn, 16)

            def load_y(j, b):
                at, used = held(j + b * (S // TB)), held(UB * (2 * j + b - 1))
                until(sp, z2_done, used)
                until(sp, yb_done, used)
                sp.dma_start(ya[b], y_b[at, :, :, :]).then_inc(in_y[b], 16)

            def body(j):
                for b in range(2):
                    if is_block(0, j, b):
                        sp.wait_ge(wo_lo, 1)
                    if is_block(3, j, b):
                        load_ffn()
                    if there(NA, j, b, 3) and not is_block(0, j, b):
                        load_x(*shift(j, b, 3))
                    if is_block(NA - 2, j, b):
                        for k in range(2):
                            sp.wait_ge(y_out[k], 16 * (TB // TA))
                        sp.wait_ge(z_done, 2 * NA)
                        load_y(0, 0)
                    if is_block(NA, j, b):
                        for k in range(2, 4):
                            sp.wait_ge(y_out[k], 16 * (TB // TA))
                        sp.wait_ge(ffn_lo[1], 1)
                        load_y(0, 1)
                    if there(NA, j, b, -2):
                        for u in range(2):
                            k = 2 * b + u
                            row = held(tile_row(j - 1, b, u))
                            sp.wait_ge(y_done, 2 * num(j, b, -2) + u + 1)
                            sp.dma_start(y_t[row, :, :], xb[:, k, :]).then_inc(y_out[k], 16)
                    if there(NA, j, b, 0):
                        for u in range(2):
                            k = 2 * b + u
                            row = held(tile_row(j, b, u))
                            until(sp, y_out[k], 16 * j)
                            sp.dma_start(xb[:, k, :], x_t[row, :, :]).then_inc(in_xb[k], 16)

            pairs(sp, NA, body)

            for k in range(4):
                sp.wait_ge(y_out[k], 16 * (NA // 2))

            def body2(j):
                for b in range(2):
                    if there(NB, j, b, 2):
                        load_y(j + 1, b)
                    if there(NB, j, b, -1):
                        jj, bb = shift(j, b, -1)
                        for t in range(UB):
                            row = held(UB * jj + (bb * TPB + t))
                            sp.wait_ge(o2_done, UB * num(j, b, -1) + t + 1)
                            sp.dma_start(out_t[row, :, :], yb[bb][:, t, :])\
                              .then_inc(outs[bb], 16)

            pairs(sp, NB, body2)
            for b in range(2):
                sp.wait_ge(outs[b], 16 * UB * (NB // 2))

        @block.gpsimd
        def _(pool):
            pool.memset(ident[:, :], 0.0).then_inc(const_ready, 1)
            pool.memset(mhalf[:, :], -0.5).then_inc(const_ready, 1)
            pool.memset(eps_c[:, :], EPS).then_inc(const_ready, 1)
            pool.wait_ge(const_ready, 3)
            pool.affine_select(out=ident[:, :], in_=ident[:, :], compare_op=ALU.not_equal, fill=1.0,
                               base=0, pattern=[[-1, P]], channel_multiplier=1).then_inc(const_ready, 1)

            def rstd_of(j, b):
                n = 2 * j + b
                pool.wait_ge(mv_done, 2 * n + 2)
                until(pool, z_done, 2 * n - 2)
                pool.tensor_tensor(var_e[:, 2 * b:2 * b + 2], mv[:, 2 * b:2 * b + 2, 1], eps_c[:, 0:2],
                                   ALU.add).then_inc(var_done, 1)
                pool.wait_ge(var_done, n + 1)
                pool.tensor_tensor(rstd[:, 2 * b:2 * b + 2], var_e[:, 2 * b:2 * b + 2], mhalf[:, 0:2],
                                   ALU.pow).then_inc(rstd_done, 1)

            pool.memset(kb_t[:, :].bitcast(F32), 0.0).then_inc(zeroed, 1)
            rstd_of(0, 0)
            pool.memset(vrows[:, :, :, :], 0.0).then_inc(zeroed, 1)
            pool.wait_ge(wq_hi, 2)
            pool.tensor_tensor(wq_half(wq_r[:, 1, :, :], 1), wq_half(wq_f, 1),
                               wq_half(wq_r[:, 0, :, :], 1).bitcast(F32), ALU.subtract).then_inc(wq_lo_pool, 1)
            rstd_of(0, 1)
            rstd_of(1, 0)
            pool.wait_ge(wo_hi, 1)
            pool.tensor_tensor(wo_r[:, 1, :, :], wo_f, wo_r[:, 0, :, :].bitcast(F32),
                               ALU.subtract).then_inc(wo_lo, 1)

            def heads(t, k):
                return t[:, k, 0:HKV].rearrange("p (h w) -> p h w", h=H)

            def subtract_max(j, b, u):
                k = 2 * b + u
                pool.wait_ge(s_max, 2 * num(j, b) + u + 1)
                pool.tensor_tensor(heads(sc, k), heads(sc, k),
                                   smax[:, k, :].unsqueeze(2).broadcast_to([P, H, KV]),
                                   ALU.subtract).then_inc(s_sub, 1)

            def normalise(j, b, u):
                k = 2 * b + u
                pool.wait_ge(s_rec, 2 * num(j, b) + u + 1)
                pool.tensor_tensor(heads(sc, k), heads(sc, k),
                                   rsum[:, k, :].unsqueeze(2).broadcast_to([P, H, KV]),
                                   ALU.mult).then_inc(s_norm, 1)

            def x_plus_bo(j, b, u):
                k = 2 * b + u
                if is_block(0, j, b) and u == 0:
                    pool.wait_ge(in_bo, 16)
                pool.wait_ge(in_xb[k], 16 * (j + 1))
                pool.tensor_tensor(xb[:, k, :], xb[:, k, :], bias_row[:, :], ALU.add).then_inc(xb_done, 1)

            def rstd2_of(j, b):
                n = 2 * j + b
                pool.wait_ge(mv2, UB * (n + 1))
                until(pool, z2_done, UB * n)
                pool.tensor_tensor(var_b[:, :, 0], mv_b[:, :, 1], eps_c[:, :], ALU.add).then_inc(var2, 1)
                pool.wait_ge(var2, n + 1)
                pool.tensor_tensor(rstd_b[:, :, 0], var_b[:, :, 0], mhalf[:, :], ALU.pow).then_inc(rstd2, 1)

            def body(j):
                for b in range(2):
                    if is_block(NA - 1, j, b):
                        rstd2_of(0, 0)
                    if there(NA, j, b, -1):
                        normalise(*shift(j, b, -1), 1)
                    if there(NA, j, b, 0):
                        subtract_max(j, b, 0)
                    if there(NA, j, b, -1):
                        x_plus_bo(*shift(j, b, -1), 0)
                        x_plus_bo(*shift(j, b, -1), 1)
                    if is_block(0, j, b):
                        normalise(0, 0, 0)
                    if there(NA, j, b, 0):
                        subtract_max(j, b, 1)
                        if not is_block(0, j, b):
                            normalise(j, b, 0)
                    if there(NA, j, b, 3):
                        rstd_of(*shift(j, b, 3))

            pairs(pool, NA, body)

            def y_plus_b2(j, b, t):
                if is_block(0, j, b) and t == 0:
                    pool.wait_ge(in_b2, 16)
                    pool.wait_ge(ffn_lo[3], 1)
                if is_block(1, j, b) and t == 0:
                    for k in range(4):
                        pool.wait_ge(y_out[k], 16 * (NA // 2))
                if t == 0:
                    pool.wait_ge(in_y[b], 16 * (j + 1))
                    until(pool, outs[b], 16 * UB * j)
                pool.tensor_tensor(yb[b][:, t, :], ya[b][:, t, :], bias_row[:, :], ALU.add).then_inc(yb_done, 1)

            for t in range(UB):
                y_plus_b2(0, 0, t)
            rstd2_of(0, 1)

            def body2(j):
                for b in range(2):
                    for c in range(NFF):
                        if c % 2 and there(NB, j, b, 0):
                            pool.wait_ge(h_hi_act, 8 * num(j, b) + c // 2 + 1)
                            pool.tensor_tensor(hs[:, c % 4, 1, :], hg[:, c % 4, :],
                                               hs[:, c % 4, 0, :].bitcast(F32), ALU.subtract)\
                                .then_inc(h_lo_pool, 1)
                        if c == 11 and there(NB, j, b, 2):
                            rstd2_of(j + 1, b)
                        if c in (12, 13, 14, 15) and there(NB, j, b, 1):
                            y_plus_b2(*shift(j, b, 1), c - 12)

            pairs(pool, NB, body2)

        @block.scalar
        def _(act):
            for row, v in ((0, bq), (G, bk), (2 * G, b1)):
                n = v.shape[0] // P
                act.dma_start(bias_f[row:row + n, :], v.rearrange("(g p) -> g p", p=P)).then_inc(in_bias, 16)
            act.dma_start(bias_row[:, :], bv.partition_broadcast(P)).then_inc(in_bv, 16)

            def turned_z(j, b):
                n = 2 * j + b
                for u, bk_ in ((0, B6), (1, B4)):
                    act.wait_ge(zt_full, 2 * n + u + 1)
                    act.activation(zt[:, 0, :, u * P:(u + 1) * P],
                                   bk_[:, :].rearrange("p (k t) -> p k t", k=KD), ACT.Copy).then_inc(zt_hi, 1)

            def q_high(j, b, half):
                n = 2 * j + b
                act.wait_ge(q_full, 2 * n + half + 1)
                for i in range(2):
                    g = 2 * half + i
                    hi = act.activation(qt[:, b, 0, g, :], B4[:, i * TA:(i + 1) * TA], ACT.Identity,
                                        bias=bq_c[:, g:g + 1])
                hi.then_inc(q_hi, 1)

            def k_high(b):
                for dst, src in k_heads(b, 0):
                    last = act.activation(dst, src, ACT.Copy)
                last.then_inc(kb_hi, 1)

            for half in range(2):
                act.wait_ge(in_wq[half], 16)
                act.activation(wq_half(wq_r[:, 0, :, :], half), wq_half(wq_f, half), ACT.Copy).then_inc(wq_hi, 1)
                if half == 0:
                    turned_z(0, 0)
            act.wait_ge(k_copied, 1)
            act.wait_ge(zeroed, 1)
            k_high(0)
            act.wait_ge(bias_ready, 1)
            q_high(0, 0, 0)
            k_high(1)
            act.wait_ge(in_wo, 16)
            act.activation(wo_r[:, 0, :, :], wo_f, ACT.Copy).then_inc(wo_hi, 1)
            q_high(0, 0, 1)
            turned_z(0, 1)

            def copy_probs(j, b, u, parts):
                s = 2 * (2 * j + b) + u
                for part in parts:
                    c0, bk_ = 4 * part, (B5, B6, B5)[part]
                    nch = min(4, NCH - c0)
                    act.wait_ge(pt_full, 3 * s + (part + 1))
                    act.activation(pt[:, c0:c0 + nch, u * P:(u + 1) * P],
                                   bk_[:, 0:nch * P].rearrange("p (c t) -> p c t", c=nch),
                                   ACT.Copy).then_inc(pt_copied, 1)

            def exponent(j, b, u):
                k = 2 * b + u
                act.wait_ge(s_sub, 2 * num(j, b) + u + 1)
                act.activation(sc[:, k, 0:HKV], sc[:, k, 0:HKV], ACT.Exp).then_inc(s_exp, 1)

            def heads_high(j, b):
                n = 2 * j + b
                for half, bk_ in ((0, B5), (1, B6)):
                    act.wait_ge(pv_full, 2 * n + half + 1)
                    act.activation(ot[:, 0, 2 * half:2 * half + 2, :],
                                   bk_[:, :].rearrange("p (g t) -> p g t", g=2), ACT.Copy).then_inc(ot_hi, 1)

            def ffn_high(i):
                hi, src = ((u1_r[:, 0, :, :], u1_f), (v1_r[:, 0, :], v1_f), (v2_r[:, 0, :], v2_f),
                           (u2_r[:, 0, :, :], u2_f))[i]
                act.activation(hi, src, ACT.Copy).then_inc(ffn_hi[i], 1)

            def turned_z2(j, b, t):
                act.wait_ge(z2t_full, UB * (2 * j + b) + t + 1)
                act.activation(z2t[:, 0, :, t * P:(t + 1) * P],
                               z2_bank(j, b, t).rearrange("p (k t) -> p k t", k=KD),
                               ACT.Copy).then_inc(z2t_hi, 1)

            def p1_high(j, b):
                act.wait_ge(p1_full, 2 * j + b + 1)
                act.activation(p1t[:, b, 0, :], p1_bank(j, b)[:, :], ACT.Copy).then_inc(p1_hi, 1)

            def body(j):
                for b in range(2):
                    before, after = there(NA, j, b, -1), there(NA, j, b, 1)
                    for u in range(2):
                        if before:
                            copy_probs(*shift(j, b, -1), u, (0, 1))
                        if is_block(NA, j, b) and u == 0:
                            p1_high(0, 0)
                        if after:
                            q_high(*shift(j, b, 1), u)
                        if before:
                            copy_probs(*shift(j, b, -1), u, (2,))
                        if u == 0 and is_block(0, j, b):
                            act.wait_ge(v_copied, 2)
                            act.dma_start(bias_row[:, :], bo.partition_broadcast(P)).then_inc(in_bo, 16)
                        if u == 0 and there(NA, j, b, 0):
                            exponent(j, b, 0)
                    if there(NA, j, b, 2):
                        turned_z(j + 1, b)
                    if is_block(NA - 2, j, b):
                        act.wait_ge(q_full, 2 * NA)
                        act.wait_ge(in_ffn, 4 * 16)
                        ffn_high(0)
                        ffn_high(2)
                        ffn_high(3)
                    if is_block(NA - 1, j, b):
                        turned_z2(0, 0, 0)
                        turned_z2(0, 0, 1)
                    if there(NA, j, b, 0):
                        exponent(j, b, 1)
                    if is_block(NA, j, b):
                        gelu(0, 0, 0)
                        gelu(0, 0, 1)
                        act.wait_ge(xb_done, 2 * NA)
                        act.dma_start(bias_row[:, :], b2.partition_broadcast(P)).then_inc(in_b2, 16)
                    if before:
                        heads_high(*shift(j, b, -1))
                    if is_block(NA, j, b):
                        gelu(0, 0, 2)
                        gelu(0, 0, 3)
                    if is_block(NA - 1, j, b):
                        turned_z2(0, 0, 2)
                        turned_z2(0, 0, 3)
                        act.wait_ge(s_full, 2 * NA)
                        ffn_high(1)

            def gelu(j, b, c):
                n = NFF * num(j, b) + c
                act.wait_ge(h_full, n + 1)
                if not isinstance(j, int) or n >= 4:
                    if c % 2:
                        act.wait_ge(h_lo_pool, 8 * num(j, b) + (c + 1) // 2 - 2)
                    else:
                        act.wait_ge(h_lo, 8 * num(j, b) + c // 2 - 1)
                act.activation(hg[:, c % 4, :], ps_s[:, c % 4, :], ACT.Gelu_apprx_tanh,
                               bias=b1_c[:, c:c + 1]).then_inc(h_gelu, 1)

            pairs(act, NA, body)

            def q2_high(j, b):
                act.wait_ge(u2_done, NFF * (2 * j + b + 1))
                act.activation(q2t[:, 0, :], (B4, B5)[b][:, :], ACT.Copy).then_inc(q2_hi, 1)

            def body2(j):
                for b in range(2):
                    for c in range(NFF):
                        if there(NB, j, b, 0):
                            n = NFF * num(j, b) + c
                            if not early(j, b, c):
                                gelu(j, b, c)
                            if c % 2:
                                if not isinstance(j, int) or n >= 4:
                                    act.wait_ge(u2_done, n - 3)
                                act.wait_ge(h_gelu, n + 1)
                                act.activation(hs[:, c % 4, 0, :], hg[:, c % 4, :], ACT.Copy)\
                                   .then_inc(h_hi_act, 1)
                        if c == 3 and there(NB, j, b, -1):
                            q2_high(*shift(j, b, -1))
                        if c in TURNS and there(NB, j, b, 1):
                            turned_z2(*shift(j, b, 1), TURNS.index(c))
                        if c == 13 and there(NB, j, b, 1):
                            p1_high(*shift(j, b, 1))

            pairs(act, NB, body2)

        @block.vector
        def _(dve):
            def norm_stats(j, b, u):
                k = 2 * b + u
                n = 2 * (2 * j + b) + u
                dve.wait_ge(in_x[k], 16 * (j + 1))
                until(dve, z_done, n - 3)
                dve.bn_stats(stats[:, k, :], xa[:, k, :]).then_inc(stats_done, 1)
                dve.wait_ge(stats_done, n + 1)
                dve.memset(stall[:, :], 0.0)
                dve.bn_aggr(mv[:, k, :], stats[:, k, :]).then_inc(mv_done, 1)

            def norm_z(j, b):
                n = 2 * j + b
                dve.wait_ge(rstd_done, n + 1)
                for u in range(2):
                    k = 2 * b + u
                    until(dve, zt_full, 2 * n + u - 1)
                    dve.tensor_scalar(z[:, u, :], xa[:, k, :], mv[:, k, 0:1], rstd[:, k:k + 1],
                                      ALU.subtract, ALU.mult).then_inc(z_done, 1)

            def turned_z(j, b):
                n = 2 * j + b
                for u, bk_ in ((0, B6), (1, B4)):
                    dve.wait_ge(zt_hi, 2 * n + u + 1)
                    dve.tensor_tensor(zt[:, 1, :, u * P:(u + 1) * P],
                                      bk_[:, :].rearrange("p (k t) -> p k t", k=KD),
                                      zt[:, 0, :, u * P:(u + 1) * P].bitcast(F32),
                                      ALU.subtract).then_inc(zt_lo, 1)

            def q_low(j, b, half):
                n = 2 * j + b
                dve.wait_ge(q_hi, 2 * n + half + 1)
                for i in range(2):
                    g = 2 * half + i
                    lo = dve.scalar_tensor_tensor(qt[:, b, 1, g, :], B4[:, i * TA:(i + 1) * TA],
                                                  bq_c[:, g:g + 1], qt[:, b, 0, g, :].bitcast(F32),
                                                  ALU.add, ALU.subtract)
                lo.then_inc(q_lo, 1)

            def k_low(b):
                dve.wait_ge(kb_hi, b + 1)
                for (dst, src), (hi, _) in zip(k_heads(b, 1), k_heads(b, 0)):
                    last = dve.tensor_tensor(dst, src, hi.bitcast(F32), ALU.subtract)
                last.then_inc(kb_lo, 1)

            def v_sum(b):
                dve.wait_ge(v_full, b + 1)
                dve.tensor_tensor(v_f[:, b, :], (B5, B7)[b][0:KV, :], bias_row[0:KV, :],
                                  ALU.add).then_inc(v_copied, 1)

            dve.wait_ge(ctx_turned, 1)
            dve.tensor_copy(once[:, 0:KC * B * KV], B7[:, 0:KC * B * KV]).then_inc(ctx_copied, 1)
            dve.wait_ge(bias_turned, 1)
            dve.tensor_copy(bias_c[:, :], B5[:, 0:2 * G + NFF]).then_inc(bias_ready, 1)
            norm_stats(0, 0, 0)
            norm_stats(0, 0, 1)
            norm_z(0, 0)
            dve.wait_ge(wq_hi, 1)
            dve.tensor_tensor(wq_half(wq_r[:, 1, :, :], 0), wq_half(wq_f, 0),
                              wq_half(wq_r[:, 0, :, :], 0).bitcast(F32), ALU.subtract).then_inc(wq_lo, 1)
            dve.wait_ge(k_full, 1)
            dve.wait_ge(bias_ready, 1)
            for g in range(G):
                src = ps_s[:, g // 3, (g % 3) * B * KV:(g % 3 + 1) * B * KV]
                last = dve.tensor_scalar(kt_f[:, g, :, :].rearrange("p b w -> p (b w)"), src,
                                         bk_c[:, g:g + 1], SCALE, ALU.add, ALU.mult)
            last.then_inc(k_copied, 1)
            turned_z(0, 0)
            norm_stats(0, 1, 0)
            norm_stats(0, 1, 1)
            k_low(0)
            q_low(0, 0, 0)
            norm_z(0, 1)
            dve.wait_ge(in_bv, 16)
            v_sum(0)
            k_low(1)
            norm_stats(1, 0, 0)
            norm_stats(1, 0, 1)
            q_low(0, 0, 1)
            turned_z(0, 1)

            def clip(j, b, u):
                k, s = 2 * b + u, 2 * (2 * j + b) + u
                dve.wait_ge(s_full, s + 1)
                until(dve, pt_full, 3 * (s - 3))
                dve.tensor_scalar(sc[:, k, 0:HKV].rearrange("p (g w) -> p g w", g=G), ps_s[:, :, 0:GW],
                                  CLAMP, -CLAMP, ALU.min, ALU.max).then_inc(s_clip, 1)

            def heads(k):
                return sc[:, k, 0:HKV].rearrange("p (h w) -> p h w", h=H)

            def maxima(j, b, u):
                k, s = 2 * b + u, 2 * (2 * j + b) + u
                dve.wait_ge(s_clip, s + 1)
                dve.tensor_reduce(smax[:, k, :], heads(k), AX.X, ALU.max).then_inc(s_max, 1)

            def sums(j, b, u):
                k, s = 2 * b + u, 2 * (2 * j + b) + u
                dve.wait_ge(s_exp, s + 1)
                dve.tensor_reduce(ssum[:, k, :], heads(k), AX.X, ALU.add).then_inc(s_sum, 1)
                dve.wait_ge(s_sum, s + 1)
                dve.reciprocal(rsum[:, k, :], ssum[:, k, :]).then_inc(s_rec, 1)

            def heads_low(j, b):
                n = 2 * j + b
                for half, bk_ in ((0, B5), (1, B6)):
                    dve.wait_ge(ot_hi, 2 * n + half + 1)
                    dve.tensor_tensor(ot[:, 1, 2 * half:2 * half + 2, :],
                                      bk_[:, :].rearrange("p (g t) -> p g t", g=2),
                                      ot[:, 0, 2 * half:2 * half + 2, :].bitcast(F32),
                                      ALU.subtract).then_inc(ot_lo, 1)

            def y_sum(j, b, u):
                k, s = 2 * b + u, 2 * (2 * j + b) + u
                dve.wait_ge(o_full, s + 1)
                dve.wait_ge(xb_done, s + 1)
                dve.tensor_tensor(xb[:, k, :], B7[:, :], xb[:, k, :], ALU.add).then_inc(y_done, 1)

            def ffn_low(i):
                dve.wait_ge(ffn_hi[i], 1)
                lo, src, hi = ((u1_r[:, 1, :, :], u1_f, u1_r[:, 0, :, :]), (v1_r[:, 1, :], v1_f, v1_r[:, 0, :]),
                               (v2_r[:, 1, :], v2_f, v2_r[:, 0, :]), (u2_r[:, 1, :, :], u2_f, u2_r[:, 0, :, :]))[i]
                dve.tensor_tensor(lo, src, hi.bitcast(F32), ALU.subtract).then_inc(ffn_lo[i], 1)

            def norm_stats2(j, b, t):
                n = UB * (2 * j + b) + t
                dve.wait_ge(in_y[b], 16 * (j + 1))
                dve.bn_stats(stats_b[:, t, :], ya[b][:, t, :]).then_inc(stats2, 1)
                dve.wait_ge(stats2, n + 1)
                dve.memset(stall[:, :], 0.0)
                dve.bn_aggr(mv_b[:, t, :], stats_b[:, t, :]).then_inc(mv2, 1)

            def norm_z2(j, b, t):
                n = 2 * j + b
                dve.wait_ge(rstd2, n + 1)
                until(dve, z2t_full, UB * (n - 1) + t + 1)
                dve.tensor_scalar(z2[:, t, :], ya[b][:, t, :], mv_b[:, t, 0:1], rstd_b[:, t, :],
                                  ALU.subtract, ALU.mult).then_inc(z2_done, 1)

            def turned_z2(j, b, t):
                dve.wait_ge(z2t_hi, UB * (2 * j + b) + t + 1)
                dve.tensor_tensor(z2t[:, 1, :, t * P:(t + 1) * P],
                                  z2_bank(j, b, t).rearrange("p (k t) -> p k t", k=KD),
                                  z2t[:, 0, :, t * P:(t + 1) * P].bitcast(F32),
                                  ALU.subtract).then_inc(z2t_lo, 1)

            def p1_low(j, b):
                dve.wait_ge(p1_hi, 2 * j + b + 1)
                dve.tensor_tensor(p1t[:, b, 1, :], p1_bank(j, b)[:, :], p1t[:, b, 0, :].bitcast(F32),
                                  ALU.subtract).then_inc(p1_lo, 1)

            def h_split(j, b, c):
                n = NFF * num(j, b) + c
                dve.wait_ge(h_gelu, n + 1)
                if not isinstance(j, int) or n >= 4:
                    dve.wait_ge(u2_done, n - 3)
                dve.tensor_copy(hs[:, c % 4, 0, :], hg[:, c % 4, :]).then_inc(h_hi, 1)
                dve.wait_ge(h_hi, 8 * num(j, b) + c // 2 + 1)
                dve.tensor_tensor(hs[:, c % 4, 1, :], hg[:, c % 4, :],
                                  hs[:, c % 4, 0, :].bitcast(F32), ALU.subtract).then_inc(h_lo, 1)

            def body(j):
                for b in range(2):
                    here, before, after = there(NA, j, b, 0), there(NA, j, b, -1), there(NA, j, b, 1)
                    for u in range(2):
                        if here:
                            clip(j, b, u)
                        if is_block(0, j, b) and u == 1:
                            q_low(0, 1, 1)
                        if here:
                            maxima(j, b, u)
                        if u == 0 and is_block(0, j, b):
                            v_sum(1)
                            for k in range(4):
                                last = dve.memset(sc[:, k, HKV:], 0.0)
                            last.then_inc(pad_zero, 1)
                        if u == 1 and here and not is_block(0, j, b):
                            sums(j, b, 0)
                        if after and not (is_block(0, j, b) and u == 1):
                            q_low(*shift(j, b, 1), u)
                        if u == 0 and is_block(0, j, b):
                            sums(0, 0, 0)
                        if u == 0 and there(NA, j, b, 2):
                            norm_z(j + 1, b)
                        if is_block(NA, j, b) and u == 0:
                            p1_low(0, 0)
                        if there(NA, j, b, -2):
                            y_sum(j - 1, b, u)
                        if is_block(NA + 1, j, b) and u == 0:
                            h_split(0, 0, 2)
                        if there(NA, j, b, 3):
                            norm_stats(*shift(j, b, 3), u)
                        if u == 0 and is_block(NA - 1, j, b):
                            for t in range(UB):
                                norm_z2(0, 0, t)
                    if there(NA, j, b, 2):
                        turned_z(j + 1, b)
                    if is_block(NA - 2, j, b):
                        for t in range(UB):
                            norm_stats2(0, 0, t)
                        ffn_low(0)
                        ffn_low(2)
                        ffn_low(3)
                    if is_block(NA - 1, j, b):
                        turned_z2(0, 0, 0)
                        turned_z2(0, 0, 1)
                    if here:
                        sums(j, b, 1)
                    if is_block(NA, j, b):
                        for t in range(UB):
                            norm_stats2(0, 1, t)
                    if before:
                        heads_low(*shift(j, b, -1))
                    if is_block(NA - 1, j, b):
                        turned_z2(0, 0, 2)
                        turned_z2(0, 0, 3)
                        ffn_low(1)
                    if is_block(NA, j, b):
                        h_split(0, 0, 0)

            pairs(dve, NA, body)

            def q2_low(j, b):
                dve.wait_ge(q2_hi, 2 * j + b + 1)
                dve.tensor_tensor(q2t[:, 1, :], (B4, B5)[b][:, :], q2t[:, 0, :].bitcast(F32),
                                  ALU.subtract).then_inc(q2_lo, 1)

            def out_sum(j, b, t):
                n = UB * (2 * j + b) + t
                dve.wait_ge(o2_full, n + 1)
                dve.wait_ge(yb_done, n + 1)
                dve.tensor_tensor(yb[b][:, t, :], B7[:, :], yb[b][:, t, :],
                                  ALU.add).then_inc(o2_done, 1)

            for t in range(UB):
                norm_z2(0, 1, t)

            def body2(j):
                for b in range(2):
                    for c in range(NFF):
                        if there(NB, j, b, 0):
                            if c % 2 == 0 and not early(j, b, c):
                                h_split(j, b, c)
                        if c == 3 and there(NB, j, b, -1):
                            q2_low(*shift(j, b, -1))
                        if c in TURNS and there(NB, j, b, 1):
                            turned_z2(*shift(j, b, 1), TURNS.index(c))
                        if c in DOWNS and there(NB, j, b, -1):
                            out_sum(*shift(j, b, -1), DOWNS.index(c))
                        if c in (7, 8, 9, 10) and there(NB, j, b, 2):
                            norm_stats2(j + 1, b, c - 7)
                        if c in (12, 13, 14, 15) and there(NB, j, b, 2):
                            norm_z2(j + 1, b, c - 12)
                        if c == 13 and there(NB, j, b, 1):
                            p1_low(*shift(j, b, 1))

            pairs(dve, NB, body2)

        @block.tensor
        def _(pe):
            def product(ps, lhs, rhs, first=True, last=True):
                for i, (a, c) in enumerate(PASSES):
                    mm = pe.matmul(ps, lhs(a), rhs(c), start=first and i == 0,
                                   stop=last and i == len(PASSES) - 1)
                return mm

            def turn_z(j, b):
                n = 2 * j + b
                for u, bk_ in ((0, B6), (1, B4)):
                    pe.wait_ge(z_done, 2 * n + u + 1)
                    if u == 0:
                        if isinstance(j, int) and n < 3:
                            until(pe, zt_lo, 2 * n - 1)
                        else:
                            pe.wait_ge(pt_copied, 6 * n - 13)
                    else:
                        until(pe, q_lo, 2 * n)
                    for k in range(KD):
                        last = pe.transpose(bk_[:, k * P:(k + 1) * P], z[:, u, k * P:(k + 1) * P],
                                            ident[:, :])
                    last.then_inc(zt_full, 1)

            def project_q(j, b, half):
                n = 2 * j + b
                pe.wait_ge(zt_lo, 2 * n + 2)
                if half:
                    pe.wait_ge(q_lo, 2 * n + 1)
                for i in range(2):
                    g = 2 * half + i
                    for k in range(KD):
                        last = product(B4[:, i * TA:(i + 1) * TA],
                                       lambda a: wq_r[:, a, k, g * P:(g + 1) * P],
                                       lambda a: zt[:, a, k, :], k == 0, k == KD - 1)
                last.then_inc(q_full, 1)

            def scores(j, b, u):
                n = 2 * j + b
                pe.wait_ge(q_lo, 2 * n + 2)
                until(pe, s_clip, 2 * n + u)
                for g in range(G):
                    last = product(ps_s[:, g, 0:GW], lambda a: qt[:, b, a, g, u * P:(u + 1) * P],
                                   lambda a: kblk[:, b, a, g, :])
                last.then_inc(s_full, 1)

            def turn_probs(j, b, u, parts):
                k, n = 2 * b + u, 2 * j + b
                s = 2 * n + u
                for part in parts:
                    bk_ = (B5, B6, B5)[part]
                    if part == 0:
                        pe.wait_ge(s_norm, s + 1)
                        if u == 0 and isinstance(j, int) and n == 0:
                            pe.wait_ge(v_copied, 1)
                        elif u == 0:
                            pe.wait_ge(ot_lo, 2 * n - 1)
                        else:
                            pe.wait_ge(pt_copied, 3 * s)
                    elif part == 1 and u == 0:
                        if isinstance(j, int) and n == 0:
                            pe.wait_ge(zt_lo, 5)
                        else:
                            pe.wait_ge(ot_lo, 2 * n)
                    elif part == 2:
                        pe.wait_ge(pt_copied, 3 * s + 1)
                    for c in range(4 * part, min(4 * part + 4, NCH)):
                        last = pe.transpose(bk_[:, (c % 4) * P:(c % 4 + 1) * P],
                                            sc[:, k, c * P:(c + 1) * P], ident[:, :])
                    last.then_inc(pt_full, 1)

            def value_steps(g):
                mine = [[(q, c) for q, (hh, c) in enumerate(PIECES) if hh == h]
                        for h in range(g * GH, (g + 1) * GH)]
                for k in range(max(len(m) for m in mine)):
                    for head, m in enumerate(mine):
                        if k < len(m):
                            yield head, *m[k], k == 0, k == len(m) - 1

            def weigh_values(j, b):
                n = 2 * j + b
                pe.wait_ge(pt_copied, 6 * n + 6)
                for half, bk_ in ((0, B5), (1, B6)):
                    if half and (not isinstance(j, int) or n + 3 < NA):
                        pe.wait_ge(zt_lo, 2 * (n + 3) + 1)
                    for i in range(2):
                        for head, q, c, first, final in value_steps(2 * half + i):
                            d0 = head * DH
                            last = pe.matmul(bk_[d0:d0 + DH, i * TA:(i + 1) * TA], vrows[:, b, q, :],
                                             pt[:, c, :], start=first, stop=final)
                    last.then_inc(pv_full, 1)

            def project_out(j, b, u):
                n = 2 * j + b
                pe.wait_ge(ot_lo, 2 * n + 2)
                until(pe, y_done, 2 * n + u)
                for k in range(KD):
                    last = product(B7[:, :], lambda a: ot[:, a, k, u * P:(u + 1) * P],
                                   lambda a: wo_r[:, a, k, :], k == 0, k == KD - 1)
                last.then_inc(o_full, 1)

            def turn_z2(j, b, t):
                n = 2 * j + b
                pe.wait_ge(z2_done, UB * n + t + 1)
                if is_block(0, j, b):
                    until(pe, z2t_lo, t - 1)
                elif t == 0:
                    until(pe, p1_lo, n)
                else:
                    pe.wait_ge(z2t_lo, UB * n + t)
                for k in range(KD):
                    last = pe.transpose(z2_bank(j, b, t)[:, k * P:(k + 1) * P], z2[:, t, k * P:(k + 1) * P],
                                        ident[:, :])
                last.then_inc(z2t_full, 1)

            def project_u1(j, b):
                n = 2 * j + b
                pe.wait_ge(z2t_lo, UB * (n + 1))
                for k in range(KD):
                    last = product(p1_bank(j, b)[:, :], lambda a: u1_r[:, a, k, :], lambda a: z2t[:, a, k, :],
                                   k == 0, k == KD - 1)
                last.then_inc(p1_full, 1)

            def v_product(b):
                for k in range(KC):
                    last = pe.matmul((B5, B7)[b][0:KV, :], ctxt_f[:, k, b, :], wv_f[:, k, :],
                                     start=k == 0, stop=k == KC - 1)
                last.then_inc(v_full, 1)

            def keep_warm(n):
                for i in range(n):
                    pe.transpose(B6[:, 0:P], ident[:, :], ident[:, :])

            pe.wait_ge(const_ready, 4)
            keep_warm(12)
            pe.wait_ge(in_ctx, 16)
            for k in range(KC):
                for b in range(B):
                    o = (k * B + b) * KV
                    last = pe.transpose(B7[:, o:o + KV], ctx_f[:, b, k * P:(k + 1) * P], ident[0:KV, 0:KV])
            last.then_inc(ctx_turned, 1)
            pe.wait_ge(in_bias, 3 * 16)
            pe.transpose(B5[:, 0:2 * G + NFF], bias_f[:, :], ident[0:2 * G + NFF, 0:2 * G + NFF])\
              .then_inc(bias_turned, 1)
            keep_warm(16)
            pe.wait_ge(ctx_copied, 1)
            pe.wait_ge(in_wk, 16)
            for g in range(G):
                for k in range(KC):
                    last = pe.matmul(ps_s[:, g // 3, (g % 3) * B * KV:(g % 3 + 1) * B * KV],
                                     wk_f[:, k, g * P:(g + 1) * P],
                                     ctxt_f[:, k, :, :].rearrange("p b w -> p (b w)"),
                                     start=k == 0, stop=k == KC - 1)
            last.then_inc(k_full, 1)
            turn_z(0, 0)
            pe.wait_ge(wq_lo, 1)
            project_q(0, 0, 0)
            pe.wait_ge(in_wv, 16)
            v_product(0)
            pe.wait_ge(wq_lo_pool, 1)
            project_q(0, 0, 1)
            turn_z(0, 1)
            pe.wait_ge(kb_lo, 1)

            def hidden(j, b, c):
                n = 2 * j + b
                if c == 0:
                    pe.wait_ge(p1_lo, n + 1)
                if not isinstance(j, int) or NFF * n + c >= 4:
                    pe.wait_ge(h_gelu, NFF * n + c - 3)
                product(ps_s[:, c % 4, :], lambda a: v1_r[:, a, c * P:(c + 1) * P],
                        lambda a: p1t[:, b, a, :]).then_inc(h_full, 1)

            def project_u2(j, b, c):
                n = 2 * j + b
                if c % 2:
                    pe.wait_ge(h_lo_pool, 8 * n + (c + 1) // 2)
                else:
                    pe.wait_ge(h_lo, 8 * n + c // 2 + 1)
                if c == 0:
                    until(pe, q2_lo, n - 1)
                product((B4, B5)[b][:, :], lambda a: u2_r[:, a, c, :], lambda a: hs[:, c % 4, a, :],
                        c == 0, c == NFF - 1).then_inc(u2_done, 1)

            def body(j):
                for b in range(2):
                    here, before, after = there(NA, j, b, 0), there(NA, j, b, -1), there(NA, j, b, 1)
                    for u in range(2):
                        if is_block(1, j, b) and u == 0:
                            pe.wait_ge(kb_lo, 2)
                        if here:
                            scores(j, b, u)
                        if is_block(0, j, b) and u == 0:
                            v_product(1)
                        if before:
                            if isinstance(j, int) and num(j, b, -1) == 0 and u == 0:
                                pe.wait_ge(pad_zero, 1)
                            turn_probs(*shift(j, b, -1), u, (0, 1))
                        if is_block(NA, j, b) and u == 0:
                            pe.wait_ge(ffn_lo[0], 1)
                            project_u1(0, 0)
                            pe.wait_ge(ffn_lo[1], 1)
                        if is_block(NA, j, b) and u == 1:
                            hidden(0, 0, 1)
                        if after:
                            project_q(*shift(j, b, 1), u)
                        if before:
                            turn_probs(*shift(j, b, -1), u, (2,))
                        if there(NA, j, b, -2):
                            if isinstance(j, int) and num(j, b, -2) == 0 and u == 0:
                                pe.wait_ge(wo_lo, 1)
                                pe.wait_ge(v_copied, 2)
                            project_out(j - 1, b, u)
                        if is_block(NA, j, b) and u == 0:
                            hidden(0, 0, 0)
                        if is_block(NA + 1, j, b) and u == 0:
                            pe.wait_ge(ffn_lo[3], 1)
                            project_u2(0, 0, 0)
                    if there(NA, j, b, 2):
                        turn_z(j + 1, b)
                    if is_block(NA - 1, j, b):
                        pe.wait_ge(s_clip, 2 * NA)
                        turn_z2(0, 0, 0)
                        turn_z2(0, 0, 1)
                    if before:
                        if is_block(1, j, b):
                            pe.wait_ge(v_placed, 16 * NP)
                        weigh_values(*shift(j, b, -1))
                    if is_block(NA - 1, j, b):
                        turn_z2(0, 0, 2)
                        turn_z2(0, 0, 3)
                    if is_block(NA, j, b):
                        hidden(0, 0, 2)
                        hidden(0, 0, 3)

            pairs(pe, NA, body)

            def project_v2(j, b, t):
                n = 2 * j + b
                pe.wait_ge(q2_lo, n + 1)
                if is_block(0, j, b) and t == 0:
                    pe.wait_ge(ffn_lo[2], 1)
                    pe.wait_ge(y_done, 2 * NA)
                until(pe, o2_done, UB * n + t)
                product(B7[:, :], lambda a: q2t[:, a, t * P:(t + 1) * P],
                        lambda a: v2_r[:, a, :]).then_inc(o2_full, 1)

            def body2(j):
                for b in range(2):
                    for c in range(NFF):
                        if there(NB, j, b, 0) and not early(j, b, c):
                            hidden(j, b, c)
                        if c >= 3 and there(NB, j, b, 0) and not (is_block(0, j, b) and c == 3):
                            project_u2(j, b, c - 3)
                        if c < 3 and there(NB, j, b, -1):
                            project_u2(*shift(j, b, -1), NFF + c - 3)
                        if c in TURNS and there(NB, j, b, 1):
                            turn_z2(*shift(j, b, 1), TURNS.index(c))
                        if c in DOWNS and there(NB, j, b, -1):
                            project_v2(*shift(j, b, -1), DOWNS.index(c))
                        if c == 12 and there(NB, j, b, 1):
                            project_u1(*shift(j, b, 1))

            pairs(pe, NB, body2)


_NAMES = ["x", "ctx_768", "L0_xattn_Wq", "L0_xattn_bq", "L0_xattn_Wk", "L0_xattn_bk", "L0_xattn_Wv",
          "L0_xattn_bv", "L0_xattn_Wo", "L0_xattn_bo", "L0_ffn_U1", "L0_ffn_V1", "L0_ffn_b1",
          "L0_ffn_U2", "L0_ffn_V2", "L0_ffn_b2"]


def kernel(**inputs):
    import numpy as np
    import concourse.bacc as bacc
    from concourse.bass_utils import run_bass_kernel_spmd

    nc = bacc.Bacc("TRN2", target_bir_lowering=False, num_devices=1)
    arrays, args = {}, []
    for name in _NAMES:
        a = np.ascontiguousarray(inputs[name])
        arrays[f"in_{name}"] = a
        args.append(nc.dram_tensor(f"in_{name}", a.shape, mybir.dt.from_np(a.dtype), kind="ExternalInput").ap())
    out = nc.dram_tensor("out", inputs["x"].shape, F32, kind="ExternalOutput").ap()
    xattn_ffn(nc, *args, out)
    r = run_bass_kernel_spmd(nc, [arrays], core_ids=[0])
    return r.results[0]["out"]
```
